# Optimizing a Trainium2 kernel written in Bass

```python
import numpy as np
import jax
import jax.numpy as jnp

def _softmax(x, axis=-1):
    return jax.nn.softmax(x, axis=axis)

def _gelu(x):
    return jax.nn.gelu(x, approximate=True)

def _silu(x):
    return jax.nn.silu(x)

def _sigmoid(x):
    return jax.nn.sigmoid(x)

def _layernorm(x, axis=-1, eps=1e-05):
    m = jnp.mean(x, axis=axis, keepdims=True)
    v = jnp.var(x, axis=axis, keepdims=True)
    return (x - m) / jnp.sqrt(v + eps)

def _scatter_add(tgt, idx, src, axis=0):
    return tgt.at[idx].add(src)

def _segment_sum(src, seg, n):
    return jax.ops.segment_sum(src, seg, n)
kernel_name = 'mk_dlrm_tower_d1_rec_r8_a82cc0'

def setup_inputs(seed: int=0):
    np.random.seed(seed)
    _w = jnp.asarray

    def _rec_inputs():
        import jax
        import jax.numpy as jnp
        _tk = jax.random.key(seed)
        ids = jnp.stack([jax.random.randint(jax.random.fold_in(_tk, 200 + f), (2048,), 0, v, jnp.int32) for f, v in enumerate([1000, 1000, 12500, 1250, 125000, 1250, 1250, 1000, 12500, 1000, 12500, 1000, 12500, 1000, 1000, 12500, 1000, 12500, 1000, 1000, 12500, 1250, 12500, 1000, 1000, 1000])], axis=1)
        tbl_0 = 0.05 * jax.random.normal(jax.random.fold_in(_tk, 500 + 0), (1000, 128), jnp.float32)
        tbl_1 = 0.05 * jax.random.normal(jax.random.fold_in(_tk, 500 + 1), (1000, 128), jnp.float32)
        tbl_2 = 0.05 * jax.random.normal(jax.random.fold_in(_tk, 500 + 2), (12500, 128), jnp.float32)
        tbl_3 = 0.05 * jax.random.normal(jax.random.fold_in(_tk, 500 + 3), (1250, 128), jnp.float32)
        tbl_4 = 0.05 * jax.random.normal(jax.random.fold_in(_tk, 500 + 4), (125000, 128), jnp.float32)
        tbl_5 = 0.05 * jax.random.normal(jax.random.fold_in(_tk, 500 + 5), (1250, 128), jnp.float32)
        tbl_6 = 0.05 * jax.random.normal(jax.random.fold_in(_tk, 500 + 6), (1250, 128), jnp.float32)
        tbl_7 = 0.05 * jax.random.normal(jax.random.fold_in(_tk, 500 + 7), (1000, 128), jnp.float32)
        tbl_8 = 0.05 * jax.random.normal(jax.random.fold_in(_tk, 500 + 8), (12500, 128), jnp.float32)
        tbl_9 = 0.05 * jax.random.normal(jax.random.fold_in(_tk, 500 + 9), (1000, 128), jnp.float32)
        tbl_10 = 0.05 * jax.random.normal(jax.random.fold_in(_tk, 500 + 10), (12500, 128), jnp.float32)
        tbl_11 = 0.05 * jax.random.normal(jax.random.fold_in(_tk, 500 + 11), (1000, 128), jnp.float32)
        tbl_12 = 0.05 * jax.random.normal(jax.random.fold_in(_tk, 500 + 12), (12500, 128), jnp.float32)
        tbl_13 = 0.05 * jax.random.normal(jax.random.fold_in(_tk, 500 + 13), (1000, 128), jnp.float32)
        tbl_14 = 0.05 * jax.random.normal(jax.random.fold_in(_tk, 500 + 14), (1000, 128), jnp.float32)
        tbl_15 = 0.05 * jax.random.normal(jax.random.fold_in(_tk, 500 + 15), (12500, 128), jnp.float32)
        tbl_16 = 0.05 * jax.random.normal(jax.random.fold_in(_tk, 500 + 16), (1000, 128), jnp.float32)
        tbl_17 = 0.05 * jax.random.normal(jax.random.fold_in(_tk, 500 + 17), (12500, 128), jnp.float32)
        tbl_18 = 0.05 * jax.random.normal(jax.random.fold_in(_tk, 500 + 18), (1000, 128), jnp.float32)
        tbl_19 = 0.05 * jax.random.normal(jax.random.fold_in(_tk, 500 + 19), (1000, 128), jnp.float32)
        tbl_20 = 0.05 * jax.random.normal(jax.random.fold_in(_tk, 500 + 20), (12500, 128), jnp.float32)
        tbl_21 = 0.05 * jax.random.normal(jax.random.fold_in(_tk, 500 + 21), (1250, 128), jnp.float32)
        tbl_22 = 0.05 * jax.random.normal(jax.random.fold_in(_tk, 500 + 22), (12500, 128), jnp.float32)
        tbl_23 = 0.05 * jax.random.normal(jax.random.fold_in(_tk, 500 + 23), (1000, 128), jnp.float32)
        tbl_24 = 0.05 * jax.random.normal(jax.random.fold_in(_tk, 500 + 24), (1000, 128), jnp.float32)
        tbl_25 = 0.05 * jax.random.normal(jax.random.fold_in(_tk, 500 + 25), (1000, 128), jnp.float32)
        _rk = jax.random.fold_in(_tk, 7)
        r_dense_features = -0.000520686 + 1.00062 * jax.random.normal(jax.random.fold_in(_rk, 101), (2048, 128), jnp.float32)
        W_top1 = 0.0405887 * jax.random.normal(jax.random.fold_in(_tk, 801), (607, 512), jnp.float32)
        W_top2 = 0.0441942 * jax.random.normal(jax.random.fold_in(_tk, 802), (512, 256), jnp.float32)
        W_top3 = 0.0625 * jax.random.normal(jax.random.fold_in(_tk, 803), (256, 1), jnp.float32)
        b_top1 = jnp.zeros((512,), jnp.float32)
        b_top2 = jnp.zeros((256,), jnp.float32)
        return (r_dense_features, ids, tbl_0, tbl_1, tbl_2, tbl_3, tbl_4, tbl_5, tbl_6, tbl_7, tbl_8, tbl_9, tbl_10, tbl_11, tbl_12, tbl_13, tbl_14, tbl_15, tbl_16, tbl_17, tbl_18, tbl_19, tbl_20, tbl_21, tbl_22, tbl_23, tbl_24, tbl_25, W_top1, b_top1, W_top2, b_top2, W_top3)
    r_dense_features, ids, tbl_0, tbl_1, tbl_2, tbl_3, tbl_4, tbl_5, tbl_6, tbl_7, tbl_8, tbl_9, tbl_10, tbl_11, tbl_12, tbl_13, tbl_14, tbl_15, tbl_16, tbl_17, tbl_18, tbl_19, tbl_20, tbl_21, tbl_22, tbl_23, tbl_24, tbl_25, W_top1, b_top1, W_top2, b_top2, W_top3 = _rec_inputs()

    def _L0_rec_setup():
        import jax, jax.numpy as jnp
        import numpy as np
        B, F, D = (2048, 26, 128)
        key = jax.random.key(seed)
        k1, k2 = jax.random.split(key)
        dense_features = jax.random.normal(k1, (B, D), dtype=jnp.float32)
        sparse_values = jax.random.normal(k2, (B, F, D), dtype=jnp.float32)
        return {'dense_features': dense_features, 'sparse_values': sparse_values}
    _L0_rec_all = _L0_rec_setup()
    _L0_rec_in = {k: v for k, v in _L0_rec_all.items() if k in ()}
    del _L0_rec_all
    return {'r_dense_features': r_dense_features, 'ids': ids, 'tbl_0': tbl_0, 'tbl_1': tbl_1, 'tbl_2': tbl_2, 'tbl_3': tbl_3, 'tbl_4': tbl_4, 'tbl_5': tbl_5, 'tbl_6': tbl_6, 'tbl_7': tbl_7, 'tbl_8': tbl_8, 'tbl_9': tbl_9, 'tbl_10': tbl_10, 'tbl_11': tbl_11, 'tbl_12': tbl_12, 'tbl_13': tbl_13, 'tbl_14': tbl_14, 'tbl_15': tbl_15, 'tbl_16': tbl_16, 'tbl_17': tbl_17, 'tbl_18': tbl_18, 'tbl_19': tbl_19, 'tbl_20': tbl_20, 'tbl_21': tbl_21, 'tbl_22': tbl_22, 'tbl_23': tbl_23, 'tbl_24': tbl_24, 'tbl_25': tbl_25, 'W_top1': W_top1, 'b_top1': b_top1, 'W_top2': W_top2, 'b_top2': b_top2, 'W_top3': W_top3}

def reference(r_dense_features, ids, tbl_0, tbl_1, tbl_2, tbl_3, tbl_4, tbl_5, tbl_6, tbl_7, tbl_8, tbl_9, tbl_10, tbl_11, tbl_12, tbl_13, tbl_14, tbl_15, tbl_16, tbl_17, tbl_18, tbl_19, tbl_20, tbl_21, tbl_22, tbl_23, tbl_24, tbl_25, W_top1, b_top1, W_top2, b_top2, W_top3):
    import jax
    import jax.numpy as jnp

    def _L0_rec_ref(dense_features, sparse_values):
        import jax, jax.numpy as jnp
        import numpy as np
        B, F, D = (2048, 26, 128)
        sd = jnp.einsum('bfd,bd->bf', sparse_values, dense_features)
        ss = jnp.einsum('bfd,bgd->bfg', sparse_values, sparse_values)
        iu, ju = jnp.triu_indices(F, k=1)
        pairs = ss[:, iu, ju]
        return jnp.concatenate([dense_features, sd, pairs], axis=1)
    e = jnp.stack([tbl_0[ids[:, 0]], tbl_1[ids[:, 1]], tbl_2[ids[:, 2]], tbl_3[ids[:, 3]], tbl_4[ids[:, 4]], tbl_5[ids[:, 5]], tbl_6[ids[:, 6]], tbl_7[ids[:, 7]], tbl_8[ids[:, 8]], tbl_9[ids[:, 9]], tbl_10[ids[:, 10]], tbl_11[ids[:, 11]], tbl_12[ids[:, 12]], tbl_13[ids[:, 13]], tbl_14[ids[:, 14]], tbl_15[ids[:, 15]], tbl_16[ids[:, 16]], tbl_17[ids[:, 17]], tbl_18[ids[:, 18]], tbl_19[ids[:, 19]], tbl_20[ids[:, 20]], tbl_21[ids[:, 21]], tbl_22[ids[:, 22]], tbl_23[ids[:, 23]], tbl_24[ids[:, 24]], tbl_25[ids[:, 25]]], axis=1)
    z = _L0_rec_ref(r_dense_features, e)
    z = z.reshape(z.shape[0], -1)
    h = jnp.concatenate([z, r_dense_features], axis=1)
    h = jnp.maximum(h @ W_top1 + b_top1, 0.0)
    h = jnp.maximum(h @ W_top2 + b_top2, 0.0)
    y = h @ W_top3
    return y

_drawn_inputs = setup_inputs


def setup_inputs(seed=0):
    import zlib

    import numpy as np

    out = dict(_drawn_inputs(seed))
    spreads = {'b_top1': (0.0, 0.1), 'b_top2': (0.0, 0.1)}
    factors = {}
    for name, (base, spread) in spreads.items():
        noise = np.random.default_rng([zlib.crc32(name.encode()), seed]).standard_normal(out[name].shape)
        drawn = base * np.exp(spread * noise) if base else spread * noise
        out[name] = jnp.asarray(drawn.astype(out[name].dtype))
    for name, factor in factors.items():
        out[name] = (out[name] * factor).astype(out[name].dtype)
    return out
```

```python
from contextlib import ExitStack

import concourse.bass as bass
from concourse import mybir

F32 = mybir.dt.float32
F32R = mybir.dt.float32r
I32 = mybir.dt.int32
U32 = mybir.dt.uint32
ALU = mybir.AluOpType
ACT = mybir.ActivationFunctionType

P = 128
BATCH = 2048
D = 128
NF = 26
GROUP = 256
NGROUP = BATCH // GROUP
TILES = GROUP // P
NJ, NP = 4, 64
SLOTS = 32
VOCAB = [1000, 1000, 12500, 1250, 125000, 1250, 1250, 1000, 12500, 1000, 12500, 1000, 12500,
         1000, 1000, 12500, 1000, 12500, 1000, 1000, 12500, 1250, 12500, 1000, 1000, 1000]
NX = 8
SMALL = 1000
VC = 8
VP = SMALL // VC
PICKED = [f for f in range(NF) if VOCAB[f] == SMALL][:NX]
GATHERED = [f for f in range(NF) if f not in PICKED]
NG = len(GATHERED)
ORDER = GATHERED + PICKED
NPAIR = NF * (NF + 1) // 2
PCH = [(c, min(P, NPAIR - c)) for c in range(0, NPAIR, P)]
H1, H2 = 512, 256
M1, M2 = H1 // P, H2 // P
RING = 2
STAGE = 3
HALF = NX // 2
TRUNS = [(s, min(4, NG + 1 - s)) for s in range(0, NG + 1, 4)]
TUNITS = [(t, s, n) for t in range(TILES) for s, n in TRUNS]
GUNITS = NP // 4
GTUNITS = [list(range(f, min(f + 4, NF))) for f in range(0, NF, 4)]
ZUNIT = len(GTUNITS)
OFF = [s * NF - s * (s - 1) // 2 for s in range(NF)]
FILL = {"GRAM": [0, 1], "GT": [2, 3], "ZT": [4], "L1": [5, 6], "L2": [7]}

E_USES = [sum(u % 2 == b for u in range(len(TUNITS) + NX // 2)) for b in (0, 1)]
G_USES = GUNITS // 2
T_USES = [(ZUNIT + 2 - b + 1) // 2 for b in (0, 1)]
H_USES = [3, 2]
OHU0 = [NX // 4, NX // 4]
assert len(TUNITS) % 2 == 0 and NX % 4 == 0 and NX % RING == 0


def build(nc, dense, idx, rows, gathered_tables, picked_tables, w1p, w1a, w1b, b1, w2, b2, w3,
          ident_in, vid_in, y):
    with ExitStack() as ctx:
        def sb(name, shape, dt=F32):
            return ctx.enter_context(nc.sbuf_tensor(name, shape, dt))

        def sem(name):
            return ctx.enter_context(nc.semaphore(name))

        idx_sb = [sb(f"idx{h}", [P, TILES, NG], U32) for h in (0, 1)]
        dense_sb = [sb(f"dense{h}", [P, TILES, D]) for h in (0, 1)]
        rows_sb = [sb(f"rows{q}", [P, HALF, GROUP], I32) for q in (0, 1)]
        E = sb("E", [P, 2 * TILES, NG, D])
        ET = sb("ET", [P, NP, NJ, SLOTS])
        shared = sb("shared", [P, STAGE * VC * D])
        raw = shared[:, :].rearrange("p (n m) -> p n m", n=STAGE)
        G = shared[:, 0:NP * NF].rearrange("q (p f) -> q p f", p=NP)
        Z = shared[0:NP, NP * NF:NP * NF + NJ * NPAIR].rearrange("p (j m) -> p j m", j=NJ)
        table_hi = sb("table_hi", [P, NX, VC * D], F32R)
        table_lo = sb("table_lo", [P, NX, VC * D], F32R)
        onehot = sb("onehot", [P, RING, VC, GROUP], F32R)
        zT = sb("zT", [P, len(PCH), GROUP])
        xT = sb("xT", [P, GROUP])
        h1T = sb("h1T", [P, M1, GROUP])
        h2T = sb("h2T", [P, M2, GROUP])
        y_row = sb("y_row", [1, BATCH])
        ident = sb("ident", [P, P])
        vid = sb("vid", [P, VC])
        w1p_sb = sb("w1p_sb", [P, len(PCH), H1])
        w1d_sb = sb("w1d_sb", [P, H1])
        w1b_sb = h1T[:, 0:H1 // GROUP, :].rearrange("p a b -> p (a b)")
        w2_sb = sb("w2_sb", [P, M1, H2])
        w3_sb = sb("w3_sb", [P, M2])
        b1_sb = sb("b1_sb", [P, M1])
        b2_sb = sb("b2_sb", [P, M2])

        psE = ctx.enter_context(nc.psum_tensor("psE", [P, 2, 512], F32))
        psG = ctx.enter_context(nc.psum_tensor("psG", [P, 2, 512], F32))
        psT = ctx.enter_context(nc.psum_tensor("psT", [P, 2, 512], F32))
        psH = ctx.enter_context(nc.psum_tensor("psH", [P, 2, 512], F32))

        consts_loaded = sem("consts_loaded")
        weights_loaded = sem("weights_loaded")
        idx_loaded = [sem(f"idx_loaded{h}") for h in (0, 1)]
        dense_loaded = [sem(f"dense_loaded{h}") for h in (0, 1)]
        rows_loaded = [sem(f"rows_loaded{q}") for q in (0, 1)]
        raw_loaded = [sem(f"raw_loaded{n}") for n in range(STAGE)]
        gathered = [sem(f"gathered{n}") for n in range(2 * TILES)]
        rows_used = sem("rows_used")
        onehot_used = sem("onehot_used")
        hi_ready = sem("hi_ready")
        lo_ready = sem("lo_ready")
        w1d_ready = sem("w1d_ready")
        onehot_ready = sem("onehot_ready")
        E_full = [sem(f"E_full{b}") for b in (0, 1)]
        E_empty = [sem(f"E_empty{b}") for b in (0, 1)]
        G_full = [sem(f"G_full{b}") for b in (0, 1)]
        G_empty = [sem(f"G_empty{b}") for b in (0, 1)]
        T_full = [sem(f"T_full{b}") for b in (0, 1)]
        T_empty = [sem(f"T_empty{b}") for b in (0, 1)]
        H_full = [sem(f"H_full{b}") for b in (0, 1)]
        H_empty = [sem(f"H_empty{b}") for b in (0, 1)]
        pe_turns = sem("pe_turns")
        pool_turns = sem("pool_turns")
        y_ready = sem("y_ready")
        y_stored = sem("y_stored")

        block = ctx.enter_context(nc.Block())

        def e_before(i, h, unit):
            b = unit % 2
            return i * (2 * E_USES[b]) + (h * E_USES[b] + unit // 2 + OHU0[b])

        def t_done(i, h, unit):
            n = len(TUNITS) // 2
            return i * (2 * n) + (h * n + unit // 2 + 1)

        def picked(i, h, k):
            return i * (2 * NX) + (h * NX + k + 1)

        def g_before(i, h, unit):
            return i * (2 * G_USES) + (h * G_USES + unit // 2)

        def t_before(i, h, unit):
            b = unit % 2
            return i * (2 * T_USES[b]) + (h * T_USES[b] + unit // 2)

        def h_before(i, h, b, k):
            return i * (2 * H_USES[b]) + (h * H_USES[b] + k)

        def group_no(i, h):
            return i * 2 + h

        def et_slots(tile, s, n):
            return ET[:, :, 2 * tile:2 * tile + 2, s:s + n].rearrange("d p j f -> d f j p")

        @block.sync
        def _(sync):
            def load_gather_inputs(i, h):
                g = group_no(i, h)
                sync.dma_start(idx_sb[h][:, :, :],
                               idx[bass.ds(g * TILES, TILES), :, :].rearrange("t p f -> p t f")
                               ).then_inc(idx_loaded[h], 16)
                sync.dma_start(dense_sb[h][:, :, :],
                               dense[bass.ds(g * TILES, TILES), :, :].rearrange("t p d -> p t d")
                               ).then_inc(dense_loaded[h], 16)

            def load_rows(i, h):
                for q in (0, 1):
                    sync.wait_ge(rows_used, group_no(i, h) * 2 + (q + 1))
                    src = rows[:, q * HALF:(q + 1) * HALF, bass.ds(group_no(i, h) * GROUP, GROUP)]
                    sync.dma_start(rows_sb[q][:, :, :], src.to_broadcast([P, HALF, GROUP])
                                   ).then_inc(rows_loaded[q], 16)

            def load_raw(n):
                if n >= STAGE:
                    sync.wait_ge(lo_ready, n - STAGE + 1)
                src = picked_tables[n].rearrange("(p c) d -> p (c d)", c=VC)
                for a, b in ((0, 112), (112, VP)):
                    sync.dma_start(raw[a:b, n % STAGE, :], src[a:b, :]).then_inc(raw_loaded[n % STAGE], 16)

            load_gather_inputs(0, 0)
            load_rows(0, 0)
            load_raw(0)
            load_raw(1)
            load_gather_inputs(0, 1)
            for n in range(2, NX):
                load_raw(n)
            load_rows(0, 1)
            with sync.Fori(1, NGROUP // 2) as i:
                for h in (0, 1):
                    sync.wait_ge(E_full[1], t_done(i - 1, h, len(TUNITS) - 1))
                    load_gather_inputs(i, h)
                    load_rows(i, h)
            sync.wait_ge(y_ready, 1)
            sync.dma_start(y.rearrange("(a s) -> a s", a=1), y_row[:, :]).then_inc(y_stored, 16)
            sync.wait_ge(y_stored, 16)

        @block.gpsimd
        def _(pool):
            with pool.Fori(0, NGROUP // 2) as i:
                for h in (0, 1):
                    pool.wait_ge(idx_loaded[h], i * 16 + 16)
                    pool.sem_inc(pool_turns, 1)
                    for t in range(TILES):
                        for n in range(NG):
                            pool.indirect_dma_start(
                                out=E[:, h * TILES + t, n, :], out_offset=None, in_=gathered_tables[n],
                                in_offset=bass.IndirectOffsetOnAxis(ap=idx_sb[h][:, t, n:n + 1], axis=0),
                            ).then_inc(gathered[h * TILES + t], 16)

        @block.tensor
        def _(pe):
            def pick(k, before, made):
                b = (k // 2) % 2
                pe.wait_ge(onehot_ready, made)
                if k % 2 == 0:
                    pe.wait_ge(E_empty[b], before + 1)
                for c in range(VC):
                    for part in (table_hi, table_lo):
                        last = nc.tensor.matmul(
                            psE[:, b, (k % 2) * GROUP:(k % 2 + 1) * GROUP],
                            part[0:VP, k, c * D:(c + 1) * D], onehot[0:VP, k % RING, c, :],
                            start=(c == 0 and part is table_hi), stop=(c == VC - 1 and part is table_lo))
                last.then_inc(onehot_used, 1)

            def fill(stage, i, h, more):
                if more:
                    for k in FILL[stage]:
                        pick(k, e_before(i, h, len(TUNITS) + k // 2), picked(i, h + 1, k))

            def group(i, h, more=True):
                for u, (t, s, n) in enumerate(TUNITS):
                    if s == 0:
                        pe.wait_ge(dense_loaded[h], i * 16 + 16)
                    if s <= 1:
                        pe.wait_ge(gathered[h * TILES + t], i * (16 * NG) + 16 * NG)
                    b = u % 2
                    pe.wait_ge(E_empty[b], e_before(i, h, u) + 1)
                    for k in range(n):
                        src = dense_sb[h][:, t, :] if s + k == 0 else E[:, h * TILES + t, s + k - 1, :]
                        last = nc.tensor.transpose(psE[:, b, k * P:(k + 1) * P], src, ident[:, :])
                    last.then_inc(E_full[b], 1)

                for b in (0, 1):
                    pe.wait_ge(E_empty[b], e_before(i, h, len(TUNITS) + b) + 1)
                for u in range(GUNITS):
                    b = u % 2
                    pe.wait_ge(G_empty[b], g_before(i, h, u) + 1)
                    for k in range(4):
                        p = 4 * u + k
                        last = nc.tensor.matmul(
                            psG[:, b, k * NJ * NF:(k + 1) * NJ * NF].rearrange("m (j f) -> m j f", j=NJ),
                            ET[:, p, :, :].rearrange("d j s -> d (j s)"), ET[:, p, :, 0:NF],
                            start=True, stop=True)
                    last.then_inc(G_full[b], 1)
                fill("GRAM", i, h, more)

                for b in (0, 1):
                    pe.wait_ge(G_empty[b], g_before(i, h, GUNITS + b) + 1)
                for u, slots in enumerate(GTUNITS):
                    b = u % 2
                    pe.wait_ge(T_empty[b], t_before(i, h, u) + 1)
                    pe.sem_inc(pe_turns, 1)
                    for k, s in enumerate(slots):
                        last = nc.tensor.transpose(psT[0:NP, b, k * P:(k + 1) * P], G[:, :, s], ident[:, :])
                    last.then_inc(T_full[b], 1)
                fill("GT", i, h, more)

                for b in (0, 1):
                    pe.wait_ge(T_empty[b], t_before(i, h, ZUNIT + (b + ZUNIT) % 2) + 1)
                pe.sem_inc(pe_turns, 1)
                for u, chunks in ((ZUNIT, (0, 1)), (ZUNIT + 1, (2,))):
                    for c in chunks:
                        c0, n = PCH[c]
                        for j in range(NJ):
                            col = (c - chunks[0]) * GROUP + j * NP
                            last = nc.tensor.transpose(psT[0:n, u % 2, col:col + NP],
                                                       Z[:, j, c0:c0 + n], ident[0:NP, 0:NP])
                    last.then_inc(T_full[u % 2], 1)
                fill("ZT", i, h, more)

                for u in (ZUNIT, ZUNIT + 1):
                    pe.wait_ge(T_empty[u % 2], t_before(i, h, u) + 2)
                for b in (0, 1):
                    pe.wait_ge(H_empty[b], h_before(i, h, b, 0) + 1)
                    for k in (0, 1):
                        m = 2 * b + k
                        out = psH[:, b, k * GROUP:(k + 1) * GROUP]
                        nc.tensor.matmul(out, w1d_sb[:, m * P:(m + 1) * P], xT[:, :], start=True, stop=False)
                        for c, (c0, n) in enumerate(PCH):
                            last = nc.tensor.matmul(out, w1p_sb[0:n, c, m * P:(m + 1) * P], zT[0:n, c, :],
                                                    start=False, stop=(c == len(PCH) - 1))
                    last.then_inc(H_full[b], 1)
                fill("L1", i, h, more)

                for b in (0, 1):
                    pe.wait_ge(H_empty[b], h_before(i, h, b, 1) + 1)
                for b in range(M2):
                    for c in range(M1):
                        last = nc.tensor.matmul(psH[:, b, 0:GROUP], w2_sb[:, c, b * P:(b + 1) * P], h1T[:, c, :],
                                                start=(c == 0), stop=(c == M1 - 1))
                    last.then_inc(H_full[b], 1)
                fill("L2", i, h, more)

                pe.wait_ge(H_empty[0], h_before(i, h, 0, 2) + 1)
                pe.wait_ge(H_empty[1], h_before(i, h, 1, 2) + 1)
                for c in range(M2):
                    last = nc.tensor.matmul(psH[0:1, 0, 0:GROUP], w3_sb[:, c:c + 1], h2T[:, c, :],
                                            start=(c == 0), stop=(c == M2 - 1))
                last.then_inc(H_full[0], 1)

            for k in range(NX):
                pe.wait_ge(lo_ready, k + 1)
                pick(k, k // 4, k + 1)
            pe.wait_ge(consts_loaded, 16 * 2)
            pe.wait_ge(weights_loaded, 16 * 7)
            pe.wait_ge(w1d_ready, 1)
            with pe.Fori(0, NGROUP // 2 - 1) as i:
                group(i, 0)
                group(i, 1)
            group(NGROUP // 2 - 1, 0)
            group(NGROUP // 2 - 1, 1, more=False)

        @block.scalar
        def _(act):
            def copy_t(i, h, u):
                t, s, n = TUNITS[u]
                act.wait_ge(E_full[0], t_done(i, h, u))
                src = psE[:, 0, 0:n * P]
                if s == 0:
                    nc.scalar.activation(xT[:, t * P:(t + 1) * P], psE[:, 0, 0:P], ACT.Copy)
                nc.scalar.activation(et_slots(t, s, n), src.rearrange("d (f j p) -> d f j p", f=n, j=2),
                                     ACT.Copy).then_inc(E_empty[0], 1)

            def copy_picked(unit, done):
                b = unit % 2
                act.wait_ge(onehot_used, done + RING)
                s = NG + 1 + 2 * unit
                nc.scalar.activation(ET[:, :, :, s:s + 2].rearrange("d p j f -> d f j p"),
                                     psE[:, b, :].rearrange("d (f j p) -> d f j p", f=2, j=NJ),
                                     ACT.Copy).then_inc(E_empty[b], 1)

            def fill(stages, i, h, more):
                if more:
                    for st in stages:
                        for k in FILL[st]:
                            if k % 2:
                                copy_picked(k // 2, picked(i, h + 1, k))

            def group(i, h, more=True):
                for u in range(0, len(TUNITS), 2):
                    copy_t(i, h, u)
                for u in range(GUNITS):
                    b = u % 2
                    act.wait_ge(G_full[b], g_before(i, h, u) + 1)
                    for j in range(NJ):
                        src = psG[32 * j:32 * j + 32, b, 0:4 * NJ * NF].rearrange("m (k j f) -> m k j f", k=4, j=NJ)
                        last = nc.scalar.activation(G[32 * j:32 * j + 32, 4 * u:4 * u + 4, :], src[:, :, j, :],
                                                    ACT.Copy)
                    last.then_inc(G_empty[b], 1)
                fill(["GRAM"], i, h, more)
                for u in range(0, len(GTUNITS), 2):
                    act.wait_ge(T_full[0], t_before(i, h, u) + 1)
                    for k, s in enumerate(GTUNITS[u]):
                        src = psT[0:NP, 0, k * P:(k + 1) * P].rearrange("p (j f) -> p j f", j=NJ)
                        last = nc.scalar.activation(Z[:, :, OFF[s]:OFF[s] + NF - s], src[:, :, s + 1:NF + 1], ACT.Copy)
                    last.then_inc(T_empty[0], 1)
                fill(["GT"], i, h, more)
                act.wait_ge(T_full[0], t_before(i, h, ZUNIT + 1) + 1)
                n = PCH[2][1]
                nc.scalar.activation(zT[0:n, 2, :], psT[0:n, 0, 0:GROUP], ACT.Copy).then_inc(T_empty[0], 1)
                fill(["ZT"], i, h, more)
                act.wait_ge(H_full[0], h_before(i, h, 0, 0) + 1)
                for m in (0, 1):
                    last = nc.scalar.activation(h1T[:, m, :], psH[:, 0, m * GROUP:(m + 1) * GROUP], ACT.Relu,
                                                bias=b1_sb[:, m:m + 1])
                last.then_inc(H_empty[0], 1)
                fill(["L1"], i, h, more)
                act.wait_ge(H_full[0], h_before(i, h, 0, 1) + 1)
                nc.scalar.activation(h2T[:, 0, :], psH[:, 0, 0:GROUP], ACT.Relu,
                                     bias=b2_sb[:, 0:1]).then_inc(H_empty[0], 1)
                fill(["L2"], i, h, more)
                act.wait_ge(H_full[0], h_before(i, h, 0, 2) + 1)
                last = nc.scalar.activation(y_row[0:1, bass.ds(group_no(i, h) * GROUP, GROUP)],
                                            psH[0:1, 0, 0:GROUP], ACT.Copy)
                last.then_inc(H_empty[0], 1)
                return last

            act.dma_start(vid[:, :], vid_in).then_inc(consts_loaded, 16)
            act.dma_start(ident[:, :], ident_in).then_inc(consts_loaded, 16)
            for b in (0, 1):
                act.sem_inc(G_empty[b], 1)
                act.sem_inc(E_empty[b], 1)
            act.dma_start(w1d_sb[:, :], w1a).then_inc(weights_loaded, 16)
            act.dma_start(w1b_sb[:, :], w1b).then_inc(weights_loaded, 16)
            act.dma_start(b1_sb[:, :], b1).then_inc(weights_loaded, 16)
            act.dma_start(b2_sb[:, :], b2).then_inc(weights_loaded, 16)
            act.dma_start(w3_sb[:, :], w3).then_inc(weights_loaded, 16)
            for n in range(NX):
                act.wait_ge(raw_loaded[n % STAGE], 32 * (n // STAGE + 1))
                nc.scalar.activation(table_hi[0:VP, n, :], raw[0:VP, n % STAGE, :], ACT.Copy).then_inc(hi_ready, 1)
                if n == 1:
                    act.dma_start(w1p_sb[:, 0:2, :], w1p[0:2 * P, :].rearrange("(c p) m -> p c m", p=P)
                                  ).then_inc(weights_loaded, 16)
                    act.dma_start(w1p_sb[0:PCH[2][1], 2, :], w1p[2 * P:NPAIR, :]).then_inc(weights_loaded, 16)
                    act.dma_start(w2_sb[:, :, :], w2.rearrange("(c p) m -> p c m", p=P)).then_inc(weights_loaded, 16)
            for k in range(NX // 2):
                copy_picked(k, 2 * k + 2)
            with act.Fori(0, NGROUP // 2 - 1) as i:
                group(i, 0)
                group(i, 1)
            group(NGROUP // 2 - 1, 0)
            last = group(NGROUP // 2 - 1, 1, more=False)
            act.wait_ge(H_empty[0], h_before(NGROUP // 2 - 1, 1, 0, H_USES[0]) + 1)
            act.sem_inc(y_ready, 1)

        @block.vector
        def _(dve):
            def make_onehot(k, loads, made):
                q = k // HALF
                if k % HALF == 0:
                    dve.wait_ge(rows_loaded[q], loads)
                dve.wait_ge(onehot_used, made)
                for c in range(VC):
                    last = nc.vector.tensor_scalar(onehot[0:VP, k % RING, c, :], rows_sb[q][0:VP, k % HALF, :],
                                                   vid[0:VP, c:c + 1], None, op0=ALU.is_equal)
                last.then_inc(onehot_ready, 1)
                if k % HALF == HALF - 1:
                    dve.wait_ge(onehot_ready, made)
                    dve.sem_inc(rows_used, 1)

            def make(ks, i, h, more):
                if more:
                    for k in ks:
                        make_onehot(k, i * 32 + 16 * (h + 2), picked(i, h + 1, k))

            def group(i, h, more=True):
                for u in range(1, len(TUNITS), 2):
                    t, s, n = TUNITS[u]
                    dve.wait_ge(E_full[1], t_done(i, h, u))
                    src = psE[:, 1, 0:n * P]
                    if s == 0:
                        nc.vector.tensor_copy(xT[:, t * P:(t + 1) * P], psE[:, 1, 0:P])
                    nc.vector.tensor_copy(et_slots(t, s, n), src.rearrange("d (f j p) -> d f j p", f=n, j=2)
                                          ).then_inc(E_empty[1], 1)
                make([0, 1, 2], i, h, more)
                for u in range(1, len(GTUNITS), 2):
                    dve.wait_ge(T_full[1], t_before(i, h, u) + 1)
                    for k, s in enumerate(GTUNITS[u]):
                        src = psT[0:NP, 1, k * P:(k + 1) * P].rearrange("p (j f) -> p j f", j=NJ)
                        last = nc.vector.tensor_copy(Z[:, :, OFF[s]:OFF[s] + NF - s], src[:, :, s + 1:NF + 1])
                    last.then_inc(T_empty[1], 1)
                make([3, 4], i, h, more)
                dve.wait_ge(T_full[1], t_before(i, h, ZUNIT) + 1)
                nc.vector.tensor_copy(zT[:, 0:2, :], psT[:, 1, :].rearrange("q (c s) -> q c s", c=2)
                                      ).then_inc(T_empty[1], 1)
                make([5], i, h, more)
                dve.wait_ge(H_full[1], h_before(i, h, 1, 0) + 1)
                for m in (2, 3):
                    last = nc.vector.tensor_scalar(h1T[:, m, :], psH[:, 1, (m - 2) * GROUP:(m - 1) * GROUP],
                                                   b1_sb[:, m:m + 1], 0.0, op0=ALU.add, op1=ALU.max)
                last.then_inc(H_empty[1], 1)
                make([6, 7], i, h, more)
                dve.wait_ge(H_full[1], h_before(i, h, 1, 1) + 1)
                nc.vector.tensor_scalar(h2T[:, 1, :], psH[:, 1, 0:GROUP], b2_sb[:, 1:2], 0.0,
                                        op0=ALU.add, op1=ALU.max).then_inc(H_empty[1], 1)

            dve.sem_inc(rows_used, 2)
            dve.sem_inc(onehot_used, RING)
            for b in (0, 1):
                dve.sem_inc(T_empty[b], 1)
                dve.sem_inc(H_empty[b], 1)
            nc.vector.memset(ET[:, :, :, NF + 1:SLOTS], 0.0)
            dve.wait_ge(consts_loaded, 32)
            for n in range(NX):
                make_onehot(n, 16, n + 1)
                dve.wait_ge(hi_ready, n + 1)
                nc.vector.tensor_tensor(table_lo[0:VP, n, :], raw[0:VP, n % STAGE, :],
                                        table_hi[0:VP, n, :].bitcast(F32), op=ALU.subtract).then_inc(lo_ready, 1)
            dve.wait_ge(weights_loaded, 16 * 8)
            nc.vector.tensor_tensor(w1d_sb[:, :], w1d_sb[:, :], w1b_sb[:, :], op=ALU.add).then_inc(w1d_ready, 1)
            with dve.Fori(0, NGROUP // 2 - 1) as i:
                group(i, 0)
                group(i, 1)
            group(NGROUP // 2 - 1, 0)
            group(NGROUP // 2 - 1, 1, more=False)


def _pair_row(a, b):
    f, g = min(a, b), max(a, b)
    return D + NF + f * (2 * NF - f - 1) // 2 + g - f - 1


def kernel(**inputs):
    import numpy as np
    import concourse.bacc as bacc
    from concourse.bass_utils import run_bass_kernel_spmd

    ids = np.ascontiguousarray(inputs["ids"])
    w1 = np.ascontiguousarray(inputs["W_top1"])
    order = [D + f for f in ORDER]
    for a in range(NF):
        order += [_pair_row(ORDER[a], ORDER[b]) for b in range(a + 1, NF)]
    vid = (VC * np.arange(P)[:, None] + np.arange(VC)[None, :]).astype(np.float32)
    host = {
        "dense": np.ascontiguousarray(inputs["r_dense_features"]).reshape(BATCH // P, P, D),
        "idx": np.ascontiguousarray(ids[:, GATHERED]).reshape(BATCH // P, P, NG),
        "rows": np.ascontiguousarray(ids[:, PICKED].T).reshape(1, NX, BATCH),
        "w1p": np.ascontiguousarray(w1[order]),
        "w1a": np.ascontiguousarray(w1[:D]),
        "w1b": np.ascontiguousarray(w1[-D:]),
        "b1": np.ascontiguousarray(np.asarray(inputs["b_top1"]).reshape(M1, P).T),
        "w2": np.ascontiguousarray(inputs["W_top2"]),
        "b2": np.ascontiguousarray(np.asarray(inputs["b_top2"]).reshape(M2, P).T),
        "w3": np.ascontiguousarray(np.asarray(inputs["W_top3"]).reshape(M2, P).T),
        "ident": np.eye(P, dtype=np.float32),
        "vid": vid,
    }
    for f in range(NF):
        host[f"tbl_{f}"] = np.ascontiguousarray(inputs[f"tbl_{f}"])
    nc = bacc.Bacc("TRN2", target_bir_lowering=False, num_devices=1)
    ap = {k: nc.dram_tensor(f"in_{k}", a.shape, mybir.dt.from_np(a.dtype), kind="ExternalInput").ap()
          for k, a in host.items()}
    y = nc.dram_tensor("y", (BATCH,), F32, kind="ExternalOutput").ap()
    build(nc, ap["dense"], ap["idx"].bitcast(U32), ap["rows"],
          [ap[f"tbl_{f}"] for f in GATHERED], [ap[f"tbl_{f}"] for f in PICKED],
          ap["w1p"], ap["w1a"], ap["w1b"], ap["b1"], ap["w2"], ap["b2"], ap["w3"], ap["ident"], ap["vid"], y)
    r = run_bass_kernel_spmd(nc, [{f"in_{k}": a for k, a in host.items()}], core_ids=[0])
    return r.results[0]["y"].reshape(BATCH, 1)
```

```python
from contextlib import ExitStack

import concourse.bass as bass
from concourse import mybir

F32 = mybir.dt.float32
F32R = mybir.dt.float32r
I32 = mybir.dt.int32
U32 = mybir.dt.uint32
ALU = mybir.AluOpType
ACT = mybir.ActivationFunctionType

P = 128
BATCH = 2048
D = 128
NF = 26
GROUP = 256
NGROUP = BATCH // GROUP
TILES = GROUP // P
NJ, NP = 4, 64
NQ = NP // TILES
SLOTS = 32
VOCAB = [1000, 1000, 12500, 1250, 125000, 1250, 1250, 1000, 12500, 1000, 12500, 1000, 12500,
         1000, 1000, 12500, 1000, 12500, 1000, 1000, 12500, 1250, 12500, 1000, 1000, 1000]
NX = 7
SMALL = 1000
VC = 8
VP = SMALL // VC
PICKED = [f for f in range(NF) if VOCAB[f] == SMALL][:NX]
GATHERED = [f for f in range(NF) if f not in PICKED]
NG = len(GATHERED)
ORDER = GATHERED + PICKED
NPAIR = NF * (NF + 1) // 2
PCH = [(c, min(P, NPAIR - c)) for c in range(0, NPAIR, P)]
OFF = [s * NF - s * (s - 1) // 2 for s in range(NF)]
H1, H2 = 512, 256
M1, M2 = H1 // P, H2 // P
RING = 4
STAGE = 3
HALF = (NX + 1) // 2

TRUNS = [(s, min(4, NG + 1 - s)) for s in range(0, NG + 1, 4)]
TUNITS = [(t, s, n) for t in range(TILES) for s, n in TRUNS]
GUNITS = NP // 4
GTUNITS = [list(range(f, min(f + 4, NF))) for f in range(0, NF, 4)]
PICK_UNITS = [list(range(k, min(k + 2, NX))) for k in range(0, NX, 2)]
FILL = {"G": [0], "GT": [1, 2], "ZT": [3], "L1": [4], "L2": [5], "L3": [6]}

E0, E1, G0, G1, T0, T1, H0, H1B = range(8)
BANK = {("T", u): (E0, E1, T0, T1)[u % 4] for u in range(len(TUNITS))}
BANK |= {("G", u): (G0, G1, H0, H1B)[u % 4] for u in range(GUNITS)}
BANK |= {("GT", u): (T0, T1, G0, G1)[u % 4] for u in range(len(GTUNITS))}
BANK |= {("ZT", 0): G1, ("ZT", 1): T0, ("L1", 0): H0, ("L1", 1): H1B, ("L2", 0): H0, ("L2", 1): H1B, ("L3", 0): H0}
BANK |= {("PICK", u): (E0, E1)[u % 2] for u in range(len(PICK_UNITS))}
USES = list(BANK)
BEFORE = {use: sum(BANK[o] == BANK[use] for o in USES[:n]) for n, use in enumerate(USES)}
PER_GROUP = [sum(BANK[o] == b for o in USES) for b in range(8)]
EARLY = [sum(BANK[o] == b for o in USES if o[0] == "PICK") for b in range(8)]
FULL_PER_GROUP = [n - early for n, early in zip(PER_GROUP, EARLY)]


def build(nc, dense, idx, rows, gathered_tables, picked_tables, w1p, w1a, w1b, b1, w2, b2, w3,
          ident_in, vid_in, y):
    with ExitStack() as ctx:
        def sb(name, shape, dt=F32):
            return ctx.enter_context(nc.sbuf_tensor(name, shape, dt))

        def sem(name):
            return ctx.enter_context(nc.semaphore(name))

        idx_sb = [sb(f"idx{h}", [P, TILES, NG], U32) for h in (0, 1)]
        dense_sb = [sb(f"dense{h}", [P, TILES, D]) for h in (0, 1)]
        rows_sb = [sb(f"rows{q}", [P, HALF, GROUP], I32) for q in (0, 1)]
        E = sb("E", [P, 2 * TILES, NG, D])
        ET = sb("ET", [P, NP, NJ, SLOTS])
        shared = sb("shared", [P, max(STAGE * VC * D, NP * NF + BATCH)])
        raw = shared[:, 0:STAGE * VC * D].rearrange("p (n m) -> p n m", n=STAGE)
        G = shared[:, 0:NP * NF].rearrange("q (p f) -> q p f", p=NP)
        Z = shared[0:NP, NP * NF:NP * NF + NJ * NPAIR].rearrange("p (j m) -> p j m", j=NJ)
        y_row = shared[NP:NP + 1, NP * NF:NP * NF + BATCH]
        table_hi = sb("table_hi", [P, NX, VC * D], F32R)
        table_lo = sb("table_lo", [P, NX, VC * D], F32R)
        onehot = sb("onehot", [P, RING, VC, GROUP], F32R)
        zT = sb("zT", [P, len(PCH), GROUP])
        xT = sb("xT", [P, GROUP])
        h1T = sb("h1T", [P, M1, GROUP])
        h2T = sb("h2T", [P, M2, GROUP])
        ident = sb("ident", [P, P])
        vid = sb("vid", [P, VC])
        w1p_sb = sb("w1p_sb", [P, len(PCH), H1])
        w1d_sb = sb("w1d_sb", [P, H1])
        w1b_sb = h1T[:, 0:H1 // GROUP, :].rearrange("p a b -> p (a b)")
        w2_sb = sb("w2_sb", [P, M1, H2])
        w3_sb = sb("w3_sb", [P, M2])
        b1_sb = sb("b1_sb", [P, M1])
        b2_sb = sb("b2_sb", [P, M2])
        bank = [ctx.enter_context(nc.psum_tensor(f"bank_{n}", [P, 512], F32))
                for n in ("E0", "E1", "G0", "G1", "T0", "T1", "H0", "H1")]

        consts_loaded = sem("consts_loaded")
        weights_loaded = sem("weights_loaded")
        idx_loaded = [sem(f"idx_loaded{h}") for h in (0, 1)]
        dense_loaded = [sem(f"dense_loaded{h}") for h in (0, 1)]
        rows_loaded = [sem(f"rows_loaded{q}") for q in (0, 1)]
        raw_loaded = [sem(f"raw_loaded{n}") for n in range(STAGE)]
        gathered = [[sem(f"gathered{n}_{k}") for k in range(len(TRUNS))] for n in range(2 * TILES)]
        hi_ready = sem("hi_ready")
        lo_ready = sem("lo_ready")
        w1d_ready = sem("w1d_ready")
        onehot_ready = sem("onehot_ready")
        onehot_used = sem("onehot_used")
        bank_full = [sem(f"bank_full{b}") for b in range(8)]
        bank_empty = [sem(f"bank_empty{b}") for b in range(8)]
        pe_turns = sem("pe_turns")
        pool_turns = sem("pool_turns")
        y_ready = sem("y_ready")
        y_stored = sem("y_stored")

        block = ctx.enter_context(nc.Block())

        def wait_empty(eng, use, i, h):
            b = BANK[use]
            eng.wait_ge(bank_empty[b], i * (2 * PER_GROUP[b]) + (h * PER_GROUP[b] + EARLY[b] + BEFORE[use] + 1))

        def wait_copied(eng, uses, i, h):
            for use in {BANK[u]: u for u in uses}.values():
                b = BANK[use]
                eng.wait_ge(bank_empty[b], i * (2 * PER_GROUP[b]) + (h * PER_GROUP[b] + EARLY[b] + BEFORE[use] + 2))

        def wait_full(eng, use, i, h):
            b = BANK[use]
            n = FULL_PER_GROUP[b]
            eng.wait_ge(bank_full[b], i * (2 * n) + (h * n + BEFORE[use] + 1))

        def picked(i, h, k):
            return i * (2 * NX) + (h * NX + k + 1)

        def group_no(i, h):
            return i * 2 + h

        def et_slots(tile, s, n):
            return ET[:, NQ * tile:NQ * (tile + 1), :, s:s + n].rearrange("d q j f -> d f j q")

        @block.sync
        def _(sync):
            def load_gather_inputs(i, h):
                g = group_no(i, h)
                sync.dma_start(idx_sb[h][:, :, :],
                               idx[bass.ds(g * TILES, TILES), :, :].rearrange("t p f -> p t f")
                               ).then_inc(idx_loaded[h], 16)
                sync.dma_start(dense_sb[h][:, :, :],
                               dense[bass.ds(g * TILES, TILES), :, :].rearrange("t p d -> p t d")
                               ).then_inc(dense_loaded[h], 16)

            def load_rows(i, h, first=False):
                for q in (0, 1):
                    tables = range(q * HALF, min((q + 1) * HALF, NX))
                    if not first:
                        sync.wait_ge(onehot_ready, picked(i, h - 1, tables[-1]))
                    src = rows[:, tables[0]:tables[-1] + 1, bass.ds(group_no(i, h) * GROUP, GROUP)]
                    sync.dma_start(rows_sb[q][:, 0:len(tables), :], src.to_broadcast([P, len(tables), GROUP])
                                   ).then_inc(rows_loaded[q], 16)

            def load_raw(n):
                if n >= STAGE:
                    sync.wait_ge(lo_ready, n - STAGE + 1)
                src = picked_tables[n].rearrange("(p c) d -> p (c d)", c=VC)
                for a, b in ((0, 112), (112, VP)):
                    sync.dma_start(raw[a:b, n % STAGE, :], src[a:b, :]).then_inc(raw_loaded[n % STAGE], 16)

            load_gather_inputs(0, 0)
            load_raw(0)
            load_rows(0, 0, first=True)
            load_raw(1)
            load_raw(2)
            load_gather_inputs(0, 1)
            for n in range(3, NX):
                load_raw(n)
            load_rows(0, 1)
            with sync.Fori(1, NGROUP // 2) as i:
                for h in (0, 1):
                    wait_full(sync, ("T", len(TUNITS) - 1), i - 1, h)
                    load_gather_inputs(i, h)
                    load_rows(i, h)
            sync.wait_ge(y_ready, 1)
            sync.dma_start(y.rearrange("(a s) -> a s", a=1), y_row).then_inc(y_stored, 16)
            sync.wait_ge(y_stored, 16)

        @block.gpsimd
        def _(pool):
            with pool.Fori(0, NGROUP // 2) as i:
                for h in (0, 1):
                    pool.wait_ge(idx_loaded[h], i * 16 + 16)
                    pool.sem_inc(pool_turns, 1)
                    for t in range(TILES):
                        for run, (s, n) in enumerate(TRUNS):
                            for table in range(max(s, 1) - 1, s + n - 1):
                                pool.indirect_dma_start(
                                    out=E[:, h * TILES + t, table, :], out_offset=None,
                                    in_=gathered_tables[table],
                                    in_offset=bass.IndirectOffsetOnAxis(ap=idx_sb[h][:, t, table:table + 1], axis=0),
                                ).then_inc(gathered[h * TILES + t][run], 16)

        @block.tensor
        def _(pe):
            def pick(k, i, h, first=False):
                use = ("PICK", k // 2)
                pe.wait_ge(onehot_ready, picked(i, h, k))
                if k % 2 == 0 and not first:
                    wait_empty(pe, use, i, h - 1)
                for c in range(VC):
                    for part in (table_hi, table_lo):
                        last = nc.tensor.matmul(
                            bank[BANK[use]][:, (k % 2) * GROUP:(k % 2 + 1) * GROUP],
                            part[0:VP, k, c * D:(c + 1) * D], onehot[0:VP, k % RING, c, :],
                            start=(c == 0 and part is table_hi), stop=(c == VC - 1 and part is table_lo))
                last.then_inc(onehot_used, 1)

            def fill(stage, i, h, more):
                if more:
                    for k in FILL[stage]:
                        pick(k, i, h + 1)

            def transpose_rows(t, i, h):
                pe.wait_ge(dense_loaded[h], i * 16 + 16)
                for u, (tile, s, n) in enumerate(TUNITS):
                    if tile != t:
                        continue
                    tables = n - (s == 0)
                    pe.wait_ge(gathered[h * TILES + t][s // 4], i * (16 * tables) + 16 * tables)
                    wait_empty(pe, ("T", u), i, h)
                    b = BANK["T", u]
                    for k in range(n):
                        src = dense_sb[h][:, t, :] if s + k == 0 else E[:, h * TILES + t, s + k - 1, :]
                        last = nc.tensor.transpose(bank[b][:, k * P:(k + 1) * P], src, ident[:, :])
                    last.then_inc(bank_full[b], 1)

            def gram(t, i, h):
                wait_copied(pe, [("T", u) for u, (tile, _, _) in enumerate(TUNITS) if tile == t], i, h)
                for u in range(t * GUNITS // TILES, (t + 1) * GUNITS // TILES):
                    b = BANK["G", u]
                    wait_empty(pe, ("G", u), i, h)
                    for k in range(4):
                        p = 4 * u + k
                        last = nc.tensor.matmul(
                            bank[b][:, k * NJ * NF:(k + 1) * NJ * NF].rearrange("m (j f) -> m j f", j=NJ),
                            ET[:, p, :, :].rearrange("d j s -> d (j s)"), ET[:, p, :, 0:NF],
                            start=True, stop=True)
                    last.then_inc(bank_full[b], 1)

            def group(i, h, more=True):
                transpose_rows(0, i, h)
                if more:
                    transpose_rows(1, i, h)
                    gram(0, i, h)
                else:
                    gram(0, i, h)
                    transpose_rows(1, i, h)
                gram(1, i, h)
                fill("G", i, h, more)

                wait_copied(pe, [("G", u) for u in range(GUNITS)], i, h)
                for u, slots in enumerate(GTUNITS):
                    b = BANK["GT", u]
                    wait_empty(pe, ("GT", u), i, h)
                    pe.sem_inc(pe_turns, 1)
                    for k, s in enumerate(slots):
                        last = nc.tensor.transpose(bank[b][0:NP, k * P:(k + 1) * P], G[:, :, s], ident[:, :])
                    last.then_inc(bank_full[b], 1)
                fill("GT", i, h, more)

                wait_copied(pe, [("GT", u) for u in range(len(GTUNITS))], i, h)
                pe.sem_inc(pe_turns, 1)
                for u, chunks in ((0, (0, 1)), (1, (2,))):
                    b = BANK["ZT", u]
                    for c in chunks:
                        c0, n = PCH[c]
                        for j in range(NJ):
                            col = (c - chunks[0]) * GROUP + j * NP
                            last = nc.tensor.transpose(bank[b][0:n, col:col + NP],
                                                       Z[:, j, c0:c0 + n], ident[0:NP, 0:NP])
                    last.then_inc(bank_full[b], 1)
                fill("ZT", i, h, more)

                wait_copied(pe, [("ZT", 0), ("ZT", 1)], i, h)
                for u in (0, 1):
                    b = BANK["L1", u]
                    for k in (0, 1):
                        m = 2 * u + k
                        out = bank[b][:, k * GROUP:(k + 1) * GROUP]
                        nc.tensor.matmul(out, w1d_sb[:, m * P:(m + 1) * P], xT[:, :], start=True, stop=False)
                        for c, (c0, n) in enumerate(PCH):
                            last = nc.tensor.matmul(out, w1p_sb[0:n, c, m * P:(m + 1) * P], zT[0:n, c, :],
                                                    start=False, stop=(c == len(PCH) - 1))
                    last.then_inc(bank_full[b], 1)
                fill("L1", i, h, more)

                wait_copied(pe, [("L1", 0), ("L1", 1)], i, h)
                for u in range(M2):
                    b = BANK["L2", u]
                    for c in range(M1):
                        last = nc.tensor.matmul(bank[b][:, 0:GROUP], w2_sb[:, c, u * P:(u + 1) * P], h1T[:, c, :],
                                                start=(c == 0), stop=(c == M1 - 1))
                    last.then_inc(bank_full[b], 1)
                fill("L2", i, h, more)

                wait_copied(pe, [("L2", 0), ("L2", 1)], i, h)
                b = BANK["L3", 0]
                for c in range(M2):
                    last = nc.tensor.matmul(bank[b][0:1, 0:GROUP], w3_sb[:, c:c + 1], h2T[:, c, :],
                                            start=(c == 0), stop=(c == M2 - 1))
                last.then_inc(bank_full[b], 1)
                fill("L3", i, h, more)

            for k in range(NX):
                pe.wait_ge(lo_ready, k + 1)
                pick(k, 0, 0, first=(k // 2 < 2))
            pe.wait_ge(consts_loaded, 16 * 2)
            pe.wait_ge(weights_loaded, 16 * 8)
            pe.wait_ge(w1d_ready, 1)
            with pe.Fori(0, NGROUP // 2 - 1) as i:
                group(i, 0)
                group(i, 1)
            group(NGROUP // 2 - 1, 0)
            group(NGROUP // 2 - 1, 1, more=False)

        @block.scalar
        def _(act):
            def copy_rows(units, i, h):
                for u in units:
                    t, s, n = TUNITS[u]
                    b = BANK["T", u]
                    wait_full(act, ("T", u), i, h)
                    if s == 0:
                        nc.scalar.activation(xT[:, :].rearrange("d (j t q) -> d j t q", j=NJ, t=TILES)[:, :, t, :],
                                             bank[b][:, 0:P].rearrange("d (j q) -> d j q", j=NJ), ACT.Copy)
                    nc.scalar.activation(et_slots(t, s, n),
                                         bank[b][:, 0:n * P].rearrange("d (f j q) -> d f j q", f=n, j=NJ),
                                         ACT.Copy).then_inc(bank_empty[b], 1)

            def copy_picked(unit, i, h):
                ks = PICK_UNITS[unit]
                b = BANK["PICK", unit]
                act.wait_ge(onehot_used, picked(i, h, ks[-1]))
                s, n = NG + 1 + ks[0], len(ks)
                nc.scalar.activation(ET[:, :, :, s:s + n].rearrange("d p j f -> d f j p"),
                                     bank[b][:, 0:n * GROUP].rearrange("d (f j p) -> d f j p", f=n, j=NJ),
                                     ACT.Copy).then_inc(bank_empty[b], 1)

            def fill(stage, i, h, more):
                if more:
                    for unit, ks in enumerate(PICK_UNITS):
                        if ks[-1] in FILL[stage]:
                            copy_picked(unit, i, h + 1)

            def copy_gram(units, i, h):
                for u in units:
                    b = BANK["G", u]
                    wait_full(act, ("G", u), i, h)
                    for j in range(NJ):
                        src = bank[b][32 * j:32 * j + 32, 0:4 * NJ * NF].rearrange("m (k j f) -> m k j f", k=4, j=NJ)
                        last = nc.scalar.activation(G[32 * j:32 * j + 32, 4 * u:4 * u + 4, :], src[:, :, j, :],
                                                    ACT.Copy)
                    last.then_inc(bank_empty[b], 1)

            def group(i, h, more=True):
                if more:
                    copy_rows(range(0, len(TUNITS), 2), i, h)
                    copy_gram(range(GUNITS), i, h)
                else:
                    for t in range(TILES):
                        copy_rows([u for u in range(0, len(TUNITS), 2) if TUNITS[u][0] == t], i, h)
                        copy_gram(range(t * GUNITS // TILES, (t + 1) * GUNITS // TILES), i, h)
                fill("G", i, h, more)
                for u, slots in enumerate(GTUNITS):
                    b = BANK["GT", u]
                    wait_full(act, ("GT", u), i, h)
                    for k, s in enumerate(slots):
                        src = bank[b][0:NP, k * P:(k + 1) * P].rearrange("p (j f) -> p j f", j=NJ)
                        last = nc.scalar.activation(Z[:, :, OFF[s]:OFF[s] + NF - s], src[:, :, s + 1:NF + 1], ACT.Copy)
                    last.then_inc(bank_empty[b], 1)
                fill("GT", i, h, more)
                b = BANK["ZT", 1]
                wait_full(act, ("ZT", 1), i, h)
                n = PCH[2][1]
                nc.scalar.activation(zT[0:n, 2, :], bank[b][0:n, 0:GROUP], ACT.Copy).then_inc(bank_empty[b], 1)
                fill("ZT", i, h, more)
                b = BANK["L1", 0]
                wait_full(act, ("L1", 0), i, h)
                for m in (0, 1):
                    last = nc.scalar.activation(h1T[:, m, :], bank[b][:, m * GROUP:(m + 1) * GROUP], ACT.Relu,
                                                bias=b1_sb[:, m:m + 1])
                last.then_inc(bank_empty[b], 1)
                fill("L1", i, h, more)
                b = BANK["L2", 0]
                wait_full(act, ("L2", 0), i, h)
                nc.scalar.activation(h2T[:, 0, :], bank[b][:, 0:GROUP], ACT.Relu,
                                     bias=b2_sb[:, 0:1]).then_inc(bank_empty[b], 1)
                fill("L2", i, h, more)
                b = BANK["L3", 0]
                wait_full(act, ("L3", 0), i, h)
                out = y_row[:, bass.ds(group_no(i, h) * GROUP, GROUP)]
                nc.scalar.activation(out.rearrange("a (t j q) -> a j t q", t=TILES, j=NJ),
                                     bank[b][0:1, 0:GROUP].rearrange("a (j t q) -> a j t q", j=NJ, t=TILES),
                                     ACT.Copy).then_inc(bank_empty[b], 1)
                fill("L3", i, h, more)

            act.dma_start(vid[:, :], vid_in).then_inc(consts_loaded, 16)
            act.dma_start(ident[:, :], ident_in).then_inc(consts_loaded, 16)
            for b in range(8):
                act.sem_inc(bank_empty[b], 1)
            act.dma_start(w1d_sb[:, :], w1a).then_inc(weights_loaded, 16)
            act.dma_start(w1b_sb, w1b).then_inc(weights_loaded, 16)
            act.dma_start(b1_sb[:, :], b1).then_inc(weights_loaded, 16)
            act.dma_start(b2_sb[:, :], b2).then_inc(weights_loaded, 16)
            act.dma_start(w3_sb[:, :], w3).then_inc(weights_loaded, 16)
            for n in range(NX):
                act.wait_ge(raw_loaded[n % STAGE], 32 * (n // STAGE + 1))
                nc.scalar.activation(table_hi[0:VP, n, :], raw[0:VP, n % STAGE, :], ACT.Copy).then_inc(hi_ready, 1)
                if n == 1:
                    act.dma_start(w1p_sb[:, 0:2, :], w1p[0:2 * P, :].rearrange("(c p) m -> p c m", p=P)
                                  ).then_inc(weights_loaded, 16)
                    act.dma_start(w1p_sb[0:PCH[2][1], 2, :], w1p[2 * P:NPAIR, :]).then_inc(weights_loaded, 16)
                    act.dma_start(w2_sb[:, :, :], w2.rearrange("(c p) m -> p c m", p=P)).then_inc(weights_loaded, 16)
                for unit, ks in enumerate(PICK_UNITS):
                    if ks[-1] == n - 1:
                        copy_picked(unit, 0, 0)
            copy_picked(len(PICK_UNITS) - 1, 0, 0)
            with act.Fori(0, NGROUP // 2 - 1) as i:
                group(i, 0)
                group(i, 1)
            group(NGROUP // 2 - 1, 0)
            group(NGROUP // 2 - 1, 1, more=False)
            wait_copied(act, [("L3", 0)], NGROUP // 2 - 1, 1)
            act.sem_inc(y_ready, 1)

        @block.vector
        def _(dve):
            def make_onehot(k, i, h, first=False):
                q = k // HALF
                if k % HALF == 0:
                    dve.wait_ge(rows_loaded[q], i * 32 + 16 * (h + 1))
                if k >= RING:
                    dve.wait_ge(onehot_used, picked(i, h, k - RING))
                elif not first:
                    dve.wait_ge(onehot_used, picked(i, h - 1, k + RING if k + RING < NX else k))
                for c in range(VC):
                    last = nc.vector.tensor_scalar(onehot[0:VP, k % RING, c, :], rows_sb[q][0:VP, k % HALF, :],
                                                   vid[0:VP, c:c + 1], None, op0=ALU.is_equal)
                last.then_inc(onehot_ready, 1)

            def group(i, h, more=True):
                for u in range(1, len(TUNITS), 2):
                    t, s, n = TUNITS[u]
                    b = BANK["T", u]
                    wait_full(dve, ("T", u), i, h)
                    if s == 0:
                        nc.vector.tensor_copy(xT[:, :].rearrange("d (j t q) -> d j t q", j=NJ, t=TILES)[:, :, t, :],
                                              bank[b][:, 0:P].rearrange("d (j q) -> d j q", j=NJ))
                    nc.vector.tensor_copy(et_slots(t, s, n),
                                          bank[b][:, 0:n * P].rearrange("d (f j q) -> d f j q", f=n, j=NJ)
                                          ).then_inc(bank_empty[b], 1)
                if more:
                    for k in range(NX):
                        make_onehot(k, i, h + 1)
                b = BANK["ZT", 0]
                wait_full(dve, ("ZT", 0), i, h)
                nc.vector.tensor_copy(zT[:, 0:2, :], bank[b][:, :].rearrange("q (c s) -> q c s", c=2)
                                      ).then_inc(bank_empty[b], 1)
                b = BANK["L1", 1]
                wait_full(dve, ("L1", 1), i, h)
                for m in (2, 3):
                    last = nc.vector.tensor_scalar(h1T[:, m, :], bank[b][:, (m - 2) * GROUP:(m - 1) * GROUP],
                                                   b1_sb[:, m:m + 1], 0.0, op0=ALU.add, op1=ALU.max)
                last.then_inc(bank_empty[b], 1)
                b = BANK["L2", 1]
                wait_full(dve, ("L2", 1), i, h)
                nc.vector.tensor_scalar(h2T[:, 1, :], bank[b][:, 0:GROUP], b2_sb[:, 1:2], 0.0,
                                        op0=ALU.add, op1=ALU.max).then_inc(bank_empty[b], 1)

            nc.vector.memset(ET[:, :, :, NF + 1:SLOTS], 0.0)
            dve.wait_ge(consts_loaded, 32)
            for n in range(NX):
                make_onehot(n, 0, 0, first=True)
                dve.wait_ge(hi_ready, n + 1)
                nc.vector.tensor_tensor(table_lo[0:VP, n, :], raw[0:VP, n % STAGE, :],
                                        table_hi[0:VP, n, :].bitcast(F32), op=ALU.subtract).then_inc(lo_ready, 1)
            dve.wait_ge(weights_loaded, 16 * 8)
            nc.vector.tensor_tensor(w1d_sb[:, :], w1d_sb[:, :], w1b_sb, op=ALU.add).then_inc(w1d_ready, 1)
            with dve.Fori(0, NGROUP // 2 - 1) as i:
                group(i, 0)
                group(i, 1)
            group(NGROUP // 2 - 1, 0)
            group(NGROUP // 2 - 1, 1, more=False)


def _pair_row(a, b):
    f, g = min(a, b), max(a, b)
    return D + NF + f * (2 * NF - f - 1) // 2 + g - f - 1


def kernel(**inputs):
    import numpy as np
    import concourse.bacc as bacc
    from concourse.bass_utils import run_bass_kernel_spmd

    ids = np.ascontiguousarray(inputs["ids"])
    w1 = np.ascontiguousarray(inputs["W_top1"])
    order = [D + f for f in ORDER]
    for a in range(NF):
        order += [_pair_row(ORDER[a], ORDER[b]) for b in range(a + 1, NF)]
    vid = (VC * np.arange(P)[:, None] + np.arange(VC)[None, :]).astype(np.float32)
    host = {
        "dense": np.ascontiguousarray(inputs["r_dense_features"]).reshape(BATCH // P, P, D),
        "idx": np.ascontiguousarray(ids[:, GATHERED]).reshape(BATCH // P, P, NG),
        "rows": np.ascontiguousarray(ids[:, PICKED].T.reshape(NX, NGROUP, TILES, NJ, NQ).transpose(0, 1, 3, 2, 4)
                                     ).reshape(1, NX, BATCH),
        "w1p": np.ascontiguousarray(w1[order]),
        "w1a": np.ascontiguousarray(w1[:D]),
        "w1b": np.ascontiguousarray(w1[-D:]),
        "b1": np.ascontiguousarray(np.asarray(inputs["b_top1"]).reshape(M1, P).T),
        "w2": np.ascontiguousarray(inputs["W_top2"]),
        "b2": np.ascontiguousarray(np.asarray(inputs["b_top2"]).reshape(M2, P).T),
        "w3": np.ascontiguousarray(np.asarray(inputs["W_top3"]).reshape(M2, P).T),
        "ident": np.eye(P, dtype=np.float32),
        "vid": vid,
    }
    for f in range(NF):
        host[f"tbl_{f}"] = np.ascontiguousarray(inputs[f"tbl_{f}"])
    nc = bacc.Bacc("TRN2", target_bir_lowering=False, num_devices=1)
    ap = {k: nc.dram_tensor(f"in_{k}", a.shape, mybir.dt.from_np(a.dtype), kind="ExternalInput").ap()
          for k, a in host.items()}
    y = nc.dram_tensor("y", (BATCH,), F32, kind="ExternalOutput").ap()
    build(nc, ap["dense"], ap["idx"].bitcast(U32), ap["rows"],
          [ap[f"tbl_{f}"] for f in GATHERED], [ap[f"tbl_{f}"] for f in PICKED],
          ap["w1p"], ap["w1a"], ap["w1b"], ap["b1"], ap["w2"], ap["b2"], ap["w3"], ap["ident"], ap["vid"], y)
    r = run_bass_kernel_spmd(nc, [{f"in_{k}": a for k, a in host.items()}], core_ids=[0])
    return r.results[0]["y"].reshape(BATCH, 1)
```

```python
from contextlib import ExitStack

import concourse.bass as bass
from concourse import mybir

F32 = mybir.dt.float32
F32R = mybir.dt.float32r
I32 = mybir.dt.int32
U32 = mybir.dt.uint32
ALU = mybir.AluOpType
ACT = mybir.ActivationFunctionType

P = 128
BATCH = 2048
D = 128
NF = 26
GROUP = 256
NGROUP = BATCH // GROUP
TILES = GROUP // P
NJ, NP = 4, 64
NQ = NP // TILES
SLOTS = NF + 1
ROWS = NJ * SLOTS - 1
VOCAB = [1000, 1000, 12500, 1250, 125000, 1250, 1250, 1000, 12500, 1000, 12500, 1000, 12500,
         1000, 1000, 12500, 1000, 12500, 1000, 1000, 12500, 1250, 12500, 1000, 1000, 1000]
NX = 7
SMALL = 1000
VC = 8
VP = SMALL // VC
PICKED = [f for f in range(NF) if VOCAB[f] == SMALL][:NX]
GATHERED = [f for f in range(NF) if f not in PICKED]
NG = len(GATHERED)
ORDER = GATHERED + PICKED
MAIN = [range(0, 12, 2), range(1, 12, 2)]
REST = [range(12, NF, 2), range(13, NF, 2)]


def runs(slots):
    return sum(NF - s for s in slots)


NMAIN, NREST = [runs(m) for m in MAIN], [runs(r) for r in REST]
CHUNK = [NMAIN[0], NMAIN[1], NP + NREST[1]]
ZCOLS = NMAIN[0] + CHUNK[2]
REST_ROWS = [(0, NP), (NP, CHUNK[2])]
OFF = [runs(MAIN[s % 2][:s // 2]) if s in MAIN[s % 2] else
       NMAIN[0] + NP * (s % 2) + runs(range(REST[s % 2][0], s, 2)) for s in range(NF)]
H1, H2 = 512, 256
M1, M2 = H1 // P, H2 // P
RING = 3
STAGE = 3
HALF = (NX + 1) // 2

TRUNS = [(s, min(4, NG + 1 - s)) for s in range(0, NG + 1, 4)]
TUNITS = [(t, s, n) for t in range(TILES) for s, n in TRUNS]
DENSE_UNITS = [("T", u) for u, (_, s, _) in enumerate(TUNITS) if s == 0]
GUNITS = NP // 4
GTUNITS = [list(range(s, min(s + 8, NF), 2)) for s in range(0, NF, 8)]
PICK_UNITS = [list(range(k, min(k + 2, NX))) for k in range(0, NX, 2)]
FILL = {"G": [0], "L1X": [], "GT": [1, 2], "ZT": [3, 4], "L1": [5], "L2": [6]}
NT = len(TRUNS)
T_FILL = {"L1": range(NT // 2), "L2": range(NT // 2, NT)}
PROLOGUE_T = [range(0), range(0), range(0, 2), range(2, 3), range(3, 4), range(4, NT), range(0)]
LATE = 5
MIDDLE = 2

E0, E1, G0, G1, T0, T1, H0, H1B = range(8)
BANK = {("PICK", u): (E0, E1)[u % 2] for u in range(len(PICK_UNITS))}
BANK |= {("T", u): (T0, T1, G0)[u % 3] for u in range(NT)}
BANK |= {("G", u): (T0, T1, G0, G1)[u % 4] for u in range(GUNITS)}
BANK |= {("T", u): (E0, E1, H0, H1B)[(u - NT) % 4] for u in range(NT, 2 * NT)}
BANK |= {("GT", u): (T0, T1, G0, G1)[u % 4] for u in range(len(GTUNITS))}
BANK |= {("ZT", 0): T0, ("ZT", 1): T1, ("L1", 0): H0, ("L1", 1): H1B, ("L2", 0): H0, ("L2", 1): G1, ("L3", 0): H0}
USES = list(BANK)
AHEAD = {True: GUNITS // TILES - 2, False: GUNITS // TILES - 1}
BEFORE = {use: sum(BANK[o] == BANK[use] for o in USES[:n]) for n, use in enumerate(USES)}
PER_GROUP = [sum(BANK[o] == b for o in USES) for b in range(8)]
FULL_BEFORE = {use: sum(BANK[o] == BANK[use] and o[0] != "PICK" for o in USES[:n]) for n, use in enumerate(USES)}
FULL_PER_GROUP = [sum(BANK[o] == b and o[0] != "PICK" for o in USES) for b in range(8)]


def gram_steps(units):
    steps = []
    for u in units:
        steps += [(v, j) for v, j in ((u, 3), (u - 1, 1), (u, 2), (u - 1, 0)) if v in units]
    return steps + [(units[-1], 1), (units[-1], 0)]


GRAM_STEPS = {more: gram_steps(range(n)) + gram_steps(range(n, GUNITS)) for more, n in AHEAD.items()}


def build(nc, dense, idx, rows, gathered_tables, picked_tables, w1p, w1a, w1b, b1, w2, b2, w3,
          ident_in, vid_in, y):
    with ExitStack() as ctx:
        def sb(name, shape, dt=F32):
            return ctx.enter_context(nc.sbuf_tensor(name, shape, dt))

        def sem(name):
            return ctx.enter_context(nc.semaphore(name))

        idx_sb = [sb(f"idx{h}", [P, TILES, NG], U32) for h in (0, 1)]
        dense_sb = [sb(f"dense{h}", [P, TILES, D]) for h in (0, 1)]
        rows_sb = [sb(f"rows{q}", [P, n, GROUP], I32) for q, n in enumerate((HALF, NX - HALF))]
        E = sb("E", [P, 2 * TILES, NG, D])
        ET = sb("ET", [P, NP, NJ, SLOTS])
        shared = sb("shared", [P, max(STAGE * VC * D, NF * NP + NJ * ZCOLS + 2 * GROUP)])
        raw = shared[:, 0:STAGE * VC * D].rearrange("p (n m) -> p n m", n=STAGE)
        G = shared[0:ROWS, 0:NF * NP].rearrange("q (f p) -> q f p", p=NP)
        Z = shared[:, NF * NP:NF * NP + NJ * ZCOLS].rearrange("p (j m) -> p j m", j=NJ)
        y_row = shared[0:1, NF * NP + NJ * ZCOLS:NF * NP + NJ * ZCOLS + 2 * GROUP].rearrange("a (h s) -> a h s", h=2)
        table_hi = sb("table_hi", [P, NX, VC * D], F32R)
        table_lo = sb("table_lo", [P, NX, VC * D], F32R)
        onehot = sb("onehot", [P, RING, VC, GROUP], F32R)
        zT_hi = sb("zT_hi", [P, len(CHUNK), GROUP], F32R)
        zT_lo = sb("zT_lo", [P, len(CHUNK), GROUP], F32R)
        xT_hi = sb("xT_hi", [P, GROUP], F32R)
        xT_lo = sb("xT_lo", [P, GROUP], F32R)
        h1T_hi = sb("h1T_hi", [P, M1, GROUP], F32R)
        h1T_lo = sb("h1T_lo", [P, M1, GROUP], F32R)
        h1T = shared[:, 0:M1 * GROUP].rearrange("p (m s) -> p m s", m=M1)
        h2T = shared[:, M1 * GROUP:(M1 + M2) * GROUP].rearrange("p (m s) -> p m s", m=M2)
        ones = sb("ones", [P, 1])
        ident = sb("ident", [P, P])
        vid = sb("vid", [P, VC])
        w1p_hi = sb("w1p_hi", [P, len(CHUNK), H1], F32R)
        w1p_lo = sb("w1p_lo", [P, len(CHUNK), H1], F32R)
        w1d_hi = sb("w1d_hi", [P, H1], F32R)
        w1d_lo = sb("w1d_lo", [P, H1], F32R)
        w1_raw = E[:, 2 * TILES - 1, :, :].rearrange("p a b -> p (a b)")
        w1p_raw = w1_raw[:, 0:len(CHUNK) * H1].rearrange("p (c m) -> p c m", c=len(CHUNK))
        w1a_raw = w1_raw[:, 3 * H1:4 * H1]
        w2_raw = E[:, 2 * TILES - 2, 0:M1 * H2 // D, :].rearrange("p a b -> p (a b)").rearrange(
            "p (c m) -> p c m", c=M1)
        w1b_raw = E[:, 2 * TILES - 2, M1 * H2 // D:M1 * H2 // D + H1 // D, :].rearrange("p a b -> p (a b)")
        w2_hi = sb("w2_hi", [P, M1, H2], F32R)
        w2_lo = sb("w2_lo", [P, M1, H2], F32R)
        w3_sb = sb("w3_sb", [P, M2])
        b1_sb = sb("b1_sb", [P, M1])
        b2_sb = sb("b2_sb", [P, M2])
        bank = [ctx.enter_context(nc.psum_tensor(f"bank_{n}", [P, 512], F32))
                for n in ("E0", "E1", "G0", "G1", "T0", "T1", "H0", "H1")]

        consts_loaded = sem("consts_loaded")
        weights_loaded = sem("weights_loaded")
        w1_loaded = sem("w1_loaded")
        w2_loaded = sem("w2_loaded")
        idx_loaded = [sem(f"idx_loaded{h}") for h in (0, 1)]
        dense_loaded = [sem(f"dense_loaded{h}") for h in (0, 1)]
        rows_loaded = [sem(f"rows_loaded{q}") for q in (0, 1)]
        raw_loaded = [sem(f"raw_loaded{n}") for n in range(STAGE)]
        gathered = [[sem(f"gathered{n}_{k}") for k in range(len(TRUNS))] for n in range(2 * TILES)]
        hi_ready = sem("hi_ready")
        lo_ready = sem("lo_ready")
        w1d_sum = sem("w1d_sum")
        w1_hi_ready = sem("w1_hi_ready")
        w1_ready = sem("w1_ready")
        w2_hi_ready = sem("w2_hi_ready")
        w2_ready = sem("w2_ready")
        z_hi_ready = sem("z_hi_ready")
        x_hi_ready = sem("x_hi_ready")
        x_lo_ready = sem("x_lo_ready")
        h1_hi_ready = sem("h1_hi_ready")
        h1_lo_ready = sem("h1_lo_ready")
        onehot_ready = sem("onehot_ready")
        onehot_used = sem("onehot_used")
        bank_full = [sem(f"bank_full{b}") for b in range(8)]
        bank_empty = [sem(f"bank_empty{b}") for b in range(8)]
        pe_turns = sem("pe_turns")
        pool_turns = sem("pool_turns")
        block_copied = sem("block_copied")
        h2_first = sem("h2_first")
        h2_weighted = sem("h2_weighted")
        y_stored = [sem(f"y_stored{h}") for h in (0, 1)]

        block = ctx.enter_context(nc.Block())

        def wait_empty(eng, use, i, h):
            b = BANK[use]
            eng.wait_ge(bank_empty[b], i * (2 * PER_GROUP[b]) + (h * PER_GROUP[b] + BEFORE[use] + 1))

        def wait_copied(eng, uses, i, h):
            for use in {BANK[u]: u for u in uses}.values():
                b = BANK[use]
                eng.wait_ge(bank_empty[b], i * (2 * PER_GROUP[b]) + (h * PER_GROUP[b] + BEFORE[use] + 2))

        def wait_full(eng, use, i, h):
            b = BANK[use]
            n = FULL_PER_GROUP[b]
            eng.wait_ge(bank_full[b], i * (2 * n) + (h * n + FULL_BEFORE[use] + 1))

        def picked(i, h, k):
            return i * (2 * NX) + (h * NX + k + 1)

        def blocks_until(more, step):
            return sum(j > 0 for _, j in GRAM_STEPS[more][:GRAM_STEPS[more].index(step) + 1])

        def l1_out(m):
            return bank[BANK["L1", m // 2]][:, (m % 2) * GROUP:(m % 2 + 1) * GROUP]

        def zt_main():
            return bank[BANK["ZT", 0]][0:NMAIN[0], :].rearrange("m (j a p) -> m a j p", j=NJ, a=2)

        def zt_rest(a):
            r0, r1 = REST_ROWS[a]
            return bank[BANK["ZT", 1]][r0:r1, :].rearrange("m (j a p) -> m a j p", j=NJ, a=2)[:, a, :, :]

        def dot_units(engine, more):
            return [u for u in range(len(GTUNITS)) if (0 if more else u % 2) == engine]

        def copy_dots(eng, copy, units, i, h):
            for u in units:
                b = BANK["GT", u]
                wait_full(eng, ("GT", u), i, h)
                for k, s in enumerate(GTUNITS[u]):
                    for a in (0, 1):
                        src = bank[b][NP * a:NP * (a + 1), k * NJ * SLOTS:(k + 1) * NJ * SLOTS].rearrange(
                            "p (j f) -> p j f", j=NJ)
                        last = copy(Z[NP * a:NP * (a + 1), :, OFF[s + a]:OFF[s + a] + NF - s - a],
                                    src[:, :, s + a:NF])
                last.then_inc(bank_empty[b], 1)

        def group_no(i, h):
            return i * 2 + h

        def et_slots(tile, s, n):
            return ET[:, NQ * tile:NQ * (tile + 1), :, s:s + n].rearrange("d q j f -> d f j q")

        @block.sync
        def _(sync):
            def load_gather_inputs(i, h):
                g = group_no(i, h)
                sync.dma_start(idx_sb[h][:, :, :],
                               idx[bass.ds(g * TILES, TILES), :, :].rearrange("t p f -> p t f")
                               ).then_inc(idx_loaded[h], 16)
                sync.dma_start(dense_sb[h][:, :, :],
                               dense[bass.ds(g * TILES, TILES), :, :].rearrange("t p d -> p t d")
                               ).then_inc(dense_loaded[h], 16)

            def load_rows(i, h, first=False):
                for q in (0, 1):
                    tables = range(q * HALF, min((q + 1) * HALF, NX))
                    if not first:
                        sync.wait_ge(onehot_ready, picked(i, h - 1, tables[-1]))
                    src = rows[:, tables[0]:tables[-1] + 1, bass.ds(group_no(i, h) * GROUP, GROUP)]
                    sync.dma_start(rows_sb[q][:, 0:len(tables), :], src.to_broadcast([P, len(tables), GROUP])
                                   ).then_inc(rows_loaded[q], 16)

            def load_raw(n):
                if n >= STAGE:
                    sync.wait_ge(lo_ready, n - STAGE + 1)
                src = picked_tables[n].rearrange("(p c) d -> p (c d)", c=VC)
                for a, b in ((0, 112), (112, VP)):
                    sync.dma_start(raw[a:b, n % STAGE, :], src[a:b, :]).then_inc(raw_loaded[n % STAGE], 16)

            load_gather_inputs(0, 0)
            load_raw(0)
            load_rows(0, 0, first=True)
            load_raw(1)
            load_raw(2)
            load_gather_inputs(0, 1)
            for n in range(3, NX):
                load_raw(n)
            load_rows(0, 1)
            with sync.Fori(1, NGROUP // 2) as i:
                for h in (0, 1):
                    wait_full(sync, ("T", len(TUNITS) - 1), i - 1, h)
                    load_gather_inputs(i, h)
                    load_rows(i, h)
            for h in (0, 1):
                sync.wait_ge(y_stored[h], NGROUP // 2 * 16 + 1)

        @block.gpsimd
        def _(pool):
            with pool.Fori(0, NGROUP // 2) as i:
                for h in (0, 1):
                    pool.wait_ge(idx_loaded[h], i * 16 + 16)
                    pool.sem_inc(pool_turns, 1)
                    for t in range(TILES):
                        if (h, t) == (1, 0):
                            pool.wait_ge(w1_ready, 1)
                            pool.wait_ge(w2_ready, 1)
                        for run, (s, n) in enumerate(TRUNS):
                            for table in range(max(s, 1) - 1, s + n - 1):
                                pool.indirect_dma_start(
                                    out=E[:, h * TILES + t, table, :], out_offset=None,
                                    in_=gathered_tables[table],
                                    in_offset=bass.IndirectOffsetOnAxis(ap=idx_sb[h][:, t, table:table + 1], axis=0),
                                ).then_inc(gathered[h * TILES + t][run], 16)

        @block.tensor
        def _(pe):
            def pick(k, i, h, first=False):
                use = ("PICK", k // 2)
                pe.wait_ge(onehot_ready, picked(i, h, k))
                if k % 2 == 0 and not first:
                    wait_empty(pe, use, i, h)
                for c in range(VC):
                    for part in (table_hi, table_lo):
                        last = nc.tensor.matmul(
                            bank[BANK[use]][:, (k % 2) * GROUP:(k % 2 + 1) * GROUP],
                            part[0:VP, k, c * D:(c + 1) * D], onehot[0:VP, k % RING, c, :],
                            start=(c == 0 and part is table_hi), stop=(c == VC - 1 and part is table_lo))
                last.then_inc(onehot_used, 1)

            def fill(stage, i, h, more):
                if more:
                    transpose_rows(T_FILL.get(stage, ()), i, h + 1)
                    for k in FILL[stage]:
                        pick(k, i, h + 1)

            def transpose_rows(units, i, h):
                i, h = (i + 1, 0) if h == 2 else (i, h)
                for u in units:
                    t, s, n = TUNITS[u]
                    if s == 0:
                        pe.wait_ge(dense_loaded[h], i * 16 + 16)
                    tables = n - (s == 0)
                    pe.wait_ge(gathered[h * TILES + t][s // 4], i * (16 * tables) + 16 * tables)
                    wait_empty(pe, ("T", u), i, h)
                    b = BANK["T", u]
                    for k in range(n):
                        src = dense_sb[h][:, t, :] if s + k == 0 else E[:, h * TILES + t, s + k - 1, :]
                        last = nc.tensor.transpose(bank[b][:, k * P:(k + 1) * P], src, ident[:, :])
                    last.then_inc(bank_full[b], 1)

            def gram(units, i, h):
                for u in units:
                    t, first = divmod(u, GUNITS // TILES)
                    if first == 0:
                        wait_copied(pe, [("T", n) for n, unit in enumerate(TUNITS) if unit[0] == t], i, h)
                    b = BANK["G", u]
                    wait_empty(pe, ("G", u), i, h)
                    if u == 0:
                        wait_copied(pe, [("PICK", n) for n in range(len(PICK_UNITS))], i, h)
                    for k in range(4):
                        p = 4 * u + k
                        last = nc.tensor.matmul(
                            bank[b][0:ROWS, k * NJ * NF:(k + 1) * NJ * NF].rearrange("m (j f) -> m j f", j=NJ),
                            ET[:, p, :, :].rearrange("d j s -> d (j s)")[:, 1:], ET[:, p, :, 0:NF],
                            start=True, stop=True)
                    last.then_inc(bank_full[b], 1)

            def group(i, h, more=True):
                gram(range(AHEAD[more]), i, h)
                transpose_rows(range(NT, 2 * NT), i, h)
                gram(range(AHEAD[more], GUNITS), i, h)
                fill("G", i, h, more)

                pe.wait_ge(weights_loaded, 16 * 3)
                pe.wait_ge(w1_ready, 1)
                pe.wait_ge(x_lo_ready, i * 2 + (h + 1))
                for u in (0, 1):
                    wait_empty(pe, ("L1", u), i, h)
                    for m in (2 * u, 2 * u + 1):
                        for n, (w, x) in enumerate(((w1d_hi, xT_hi), (w1d_hi, xT_lo), (w1d_lo, xT_hi))):
                            nc.tensor.matmul(l1_out(m), w[:, m * P:(m + 1) * P], x[:, :],
                                             start=(m % 2 == 0 and n == 0), stop=False)
                fill("L1X", i, h, more)

                wait_copied(pe, [("G", u) for u in range(GUNITS)], i, h)
                for u, slots in enumerate(GTUNITS):
                    b = BANK["GT", u]
                    wait_empty(pe, ("GT", u), i, h)
                    pe.sem_inc(pe_turns, 1)
                    for k, s in enumerate(slots):
                        last = nc.tensor.transpose(bank[b][:, k * NJ * SLOTS:k * NJ * SLOTS + ROWS],
                                                   G[:, s:s + 2, :].rearrange("q f p -> q (f p)"),
                                                   ident[0:ROWS, 0:ROWS])
                    last.then_inc(bank_full[b], 1)
                fill("GT", i, h, more)

                main_units = [u for u, slots in enumerate(GTUNITS) if slots[0] <= MAIN[1][-1]]
                for u, (c0, n) in enumerate(((0, NMAIN[0]), (NMAIN[0], CHUNK[2]))):
                    wait_copied(pe, [("GT", v) for v in range(len(GTUNITS)) if (v in main_units) == (u == 0)], i, h)
                    pe.sem_inc(pe_turns, 1)
                    b = BANK["ZT", u]
                    for j in range(NJ):
                        last = nc.tensor.transpose(bank[b][0:n, j * P:(j + 1) * P], Z[:, j, c0:c0 + n], ident[:, :])
                    last.then_inc(bank_full[b], 1)
                fill("ZT", i, h, more)

                pe.wait_ge(z_hi_ready, i * 4 + (2 * h + 1))
                for u in (0, 1):
                    for m, c in [(2 * u + k, c) for c in range(len(CHUNK)) for k in (0, 1)]:
                        if (m, c) == (0, 2):
                            pe.wait_ge(z_hi_ready, i * 4 + (2 * h + 2))
                        n = CHUNK[c]
                        for w in (w1p_hi, w1p_lo):
                            nc.tensor.matmul(l1_out(m), w[0:n, c, m * P:(m + 1) * P], zT_hi[0:n, c, :],
                                             start=False, stop=False)
                    if u == 0:
                        wait_copied(pe, [("ZT", 0), ("ZT", 1)], i, h)
                    for m in (2 * u, 2 * u + 1):
                        for c, n in enumerate(CHUNK):
                            last = nc.tensor.matmul(l1_out(m), w1p_hi[0:n, c, m * P:(m + 1) * P], zT_lo[0:n, c, :],
                                                    start=False, stop=(m % 2 == 1 and c == len(CHUNK) - 1))
                    last.then_inc(bank_full[BANK["L1", u]], 1)
                fill("L1", i, h, more)

                pe.wait_ge(w2_ready, 1)
                for half in (0, 1):
                    chunks = (2 * half, 2 * half + 1)
                    pe.wait_ge(h1_hi_ready, i * 4 + (2 * h + half + 1))
                    if half == 0:
                        for u in range(M2):
                            wait_empty(pe, ("L2", u), i, h)
                    for u in range(M2):
                        for c in chunks:
                            for w in (w2_hi, w2_lo):
                                nc.tensor.matmul(bank[BANK["L2", u]][:, 0:GROUP], w[:, c, u * P:(u + 1) * P],
                                                 h1T_hi[:, c, :], start=(c == 0 and w is w2_hi), stop=False)
                    pe.wait_ge(h1_lo_ready, i * 4 + (2 * h + half + 1))
                    for u in range(M2):
                        b = BANK["L2", u]
                        for c in chunks:
                            last = nc.tensor.matmul(bank[b][:, 0:GROUP], w2_hi[:, c, u * P:(u + 1) * P],
                                                    h1T_lo[:, c, :], start=False, stop=(c == M1 - 1))
                        if half == 1:
                            last.then_inc(bank_full[b], 1)
                fill("L2", i, h, more)

                b = BANK["L3", 0]
                if more:
                    pe.wait_ge(h2_weighted, i * 2 + (h + 1))
                    nc.tensor.matmul(bank[b][0:1, 0:GROUP], ones[:, :], h2T[:, 1, :], start=True, stop=True
                                     ).then_inc(bank_full[b], 1)
                else:
                    for c in range(M2):
                        wait_copied(pe, [("L2", c)], i, h)
                        last = nc.tensor.matmul(bank[b][0:1, 0:GROUP], w3_sb[:, c:c + 1], h2T[:, c, :],
                                                start=(c == 0), stop=(c == M2 - 1))
                    last.then_inc(bank_full[b], 1)

            for k in range(NX):
                pe.wait_ge(lo_ready, k + 1)
                pick(k, 0, 0, first=(k // 2 < 2))
                if k == 0:
                    pe.wait_ge(consts_loaded, 16 * 2)
                transpose_rows(PROLOGUE_T[k], 0, 0)
            with pe.Fori(0, NGROUP // 2 - 1) as i:
                group(i, 0)
                group(i, 1)
            group(NGROUP // 2 - 1, 0)
            group(NGROUP // 2 - 1, 1, more=False)

        @block.scalar
        def _(act):
            def copy_rows(units, i, h):
                i, h = (i + 1, 0) if h == 2 else (i, h)
                for u in units:
                    if TUNITS[u][1] // 4 % 2:
                        continue
                    t, s, n = TUNITS[u]
                    b = BANK["T", u]
                    wait_full(act, ("T", u), i, h)
                    nc.scalar.activation(et_slots(t, s, n),
                                         bank[b][:, 0:n * P].rearrange("d (f j q) -> d f j q", f=n, j=NJ),
                                         ACT.Copy).then_inc(bank_empty[b], 1)

            def copy_picked(unit, i, h):
                ks = PICK_UNITS[unit]
                b = BANK["PICK", unit]
                act.wait_ge(onehot_used, picked(i, h, ks[-1]))
                s, n = NG + 1 + ks[0], len(ks)
                nc.scalar.activation(ET[:, :, :, s:s + n].rearrange("d p j f -> d f j p"),
                                     bank[b][:, 0:n * GROUP].rearrange("d (f j p) -> d f j p", f=n, j=NJ),
                                     ACT.Copy).then_inc(bank_empty[b], 1)

            def fill(stage, i, h, more):
                if more:
                    copy_rows(T_FILL.get(stage, ()), i, h + 1)
                    for unit, ks in enumerate(PICK_UNITS):
                        if ks[-1] in FILL[stage]:
                            copy_picked(unit, i, h + 1)

            def copy_gram(units, i, h, more):
                for u, j in gram_steps(units):
                    b = BANK["G", u]
                    rows = SLOTS * j + NF
                    src = bank[b][0:rows, 0:4 * NJ * NF].rearrange("m (k j f) -> m k j f", k=4, j=NJ)
                    if j == NJ - 1:
                        wait_full(act, ("G", u), i, h)
                    else:
                        act.wait_ge(block_copied, i * (2 * (NJ - 1) * GUNITS)
                                    + (h * (NJ - 1) * GUNITS + blocks_until(more, (u, j + 1))))
                    nc.scalar.activation(G[0:rows, :, 4 * u:4 * u + 4].rearrange("m f k -> m k f"), src[:, :, j, :],
                                         ACT.Copy).then_inc(block_copied if j else bank_empty[b], 1)

            def group(i, h, more=True):
                copy_gram(range(AHEAD[more]), i, h, more)
                copy_rows(range(NT, 2 * NT), i, h)
                wait_copied(act, DENSE_UNITS, i, h)
                nc.scalar.activation(xT_hi[:, :].rearrange("d (j p) -> d j p", j=NJ),
                                     ET[:, :, :, 0].rearrange("d p j -> d j p"), ACT.Copy).then_inc(x_hi_ready, 1)
                copy_gram(range(AHEAD[more], GUNITS), i, h, more)
                fill("G", i, h, more)
                fill("L1X", i, h, more)
                copy_dots(act, lambda out, in_: nc.scalar.activation(out, in_, ACT.Copy), dot_units(0, more), i, h)
                fill("GT", i, h, more)
                wait_full(act, ("ZT", 0), i, h)
                n = NMAIN[0]
                nc.scalar.activation(zT_hi[0:n, 0:2, :].rearrange("m a (j p) -> m a j p", j=NJ),
                                     zt_main(), ACT.Copy).then_inc(z_hi_ready, 1)
                wait_full(act, ("ZT", 1), i, h)
                for a, (r0, r1) in enumerate(REST_ROWS):
                    last = nc.scalar.activation(zT_hi[r0:r1, 2, :].rearrange("m (j p) -> m j p", j=NJ),
                                                zt_rest(a), ACT.Copy)
                last.then_inc(z_hi_ready, 1)
                fill("ZT", i, h, more)
                b = BANK["L1", 0]
                wait_full(act, ("L1", 0), i, h)
                for m in (0, 1):
                    last = nc.scalar.activation(h1T[:, m, :], l1_out(m), ACT.Relu, bias=b1_sb[:, m:m + 1])
                last.then_inc(bank_empty[b], 1)
                for u in (0, 1):
                    wait_copied(act, [("L1", u)], i, h)
                    half = slice(2 * u, 2 * u + 2)
                    nc.scalar.activation(h1T_hi[:, half, :], h1T[:, half, :], ACT.Copy).then_inc(h1_hi_ready, 1)
                fill("L1", i, h, more)
                b = BANK["L2", 0]
                wait_full(act, ("L2", 0), i, h)
                nc.scalar.activation(h2T[:, 0, :], bank[b][:, 0:GROUP], ACT.Relu,
                                     bias=b2_sb[:, 0:1]).then_inc(bank_empty[b], 1)
                fill("L2", i, h, more)
                b = BANK["L3", 0]
                wait_full(act, ("L3", 0), i, h)
                act.wait_ge(y_stored[h], i * 16 + 1)
                nc.scalar.activation(y_row[:, h, :].rearrange("a (t j q) -> a j t q", t=TILES, j=NJ),
                                     bank[b][0:1, 0:GROUP].rearrange("a (j t q) -> a j t q", j=NJ, t=TILES),
                                     ACT.Copy).then_inc(bank_empty[b], 1)
                wait_copied(act, [("L3", 0)], i, h)
                act.dma_start(y[bass.ds(group_no(i, h) * GROUP, GROUP)].rearrange("(a s) -> a s", a=1),
                              y_row[:, h, :]).then_inc(y_stored[h], 16)

            act.dma_start(vid[:, :], vid_in).then_inc(consts_loaded, 16)
            act.dma_start(ident[:, :], ident_in).then_inc(consts_loaded, 16)
            for b in range(8):
                act.sem_inc(bank_empty[b], 1)
            for h in (0, 1):
                act.sem_inc(y_stored[h], 1)
            act.dma_start(b1_sb[:, :], b1).then_inc(weights_loaded, 16)
            act.dma_start(b2_sb[:, :], b2).then_inc(weights_loaded, 16)
            act.dma_start(w3_sb[:, :], w3).then_inc(weights_loaded, 16)
            for n in range(NX):
                act.wait_ge(raw_loaded[n % STAGE], 32 * (n // STAGE + 1))
                nc.scalar.activation(table_hi[0:VP, n, :], raw[0:VP, n % STAGE, :], ACT.Copy).then_inc(hi_ready, 1)
                if n == 1:
                    act.dma_start(w1p_raw[:, :, :], w1p.rearrange("(c p) m -> p c m", p=P)).then_inc(w1_loaded, 16)
                    act.dma_start(w1a_raw, w1a).then_inc(w1_loaded, 16)
                    act.dma_start(w1b_raw, w1b).then_inc(w1_loaded, 16)
                    act.dma_start(w2_raw, w2.rearrange("(c p) m -> p c m", p=P)).then_inc(w2_loaded, 16)
                if n == NX - 2:
                    act.wait_ge(w1_loaded, 16 * 3)
                    nc.scalar.activation(w1p_hi[:, :, :], w1p_raw[:, :, :], ACT.Copy).then_inc(w1_hi_ready, 1)
                for unit, ks in enumerate(PICK_UNITS):
                    if ks[-1] == n - 1:
                        copy_picked(unit, 0, 0)
                if n > 0:
                    copy_rows(PROLOGUE_T[n - 1], 0, 0)
            copy_picked(len(PICK_UNITS) - 1, 0, 0)
            copy_rows(PROLOGUE_T[NX - 1], 0, 0)
            act.wait_ge(w1d_sum, 1)
            nc.scalar.activation(w1d_hi[:, :], w1a_raw, ACT.Copy).then_inc(w1_hi_ready, 1)
            act.wait_ge(w2_loaded, 16)
            nc.scalar.activation(w2_hi[:, :, :], w2_raw, ACT.Copy).then_inc(w2_hi_ready, 1)
            with act.Fori(0, NGROUP // 2 - 1) as i:
                group(i, 0)
                group(i, 1)
            group(NGROUP // 2 - 1, 0)
            group(NGROUP // 2 - 1, 1, more=False)

        @block.vector
        def _(dve):
            def make_onehot(k, i, h, first=False):
                q = k // HALF
                if k % HALF == 0:
                    dve.wait_ge(rows_loaded[q], i * 32 + 16 * (h + 1))
                if k >= RING:
                    dve.wait_ge(onehot_used, picked(i, h, k - RING))
                elif not first:
                    dve.wait_ge(onehot_used, picked(i, h - 1, range(k, NX, RING)[-1]))
                for c in range(VC):
                    last = nc.vector.tensor_scalar(onehot[0:VP, k % RING, c, :], rows_sb[q][0:VP, k % HALF, :],
                                                   vid[0:VP, c:c + 1], None, op0=ALU.is_equal)
                last.then_inc(onehot_ready, 1)

            def copy_rows(units, i, h):
                i, h = (i + 1, 0) if h == 2 else (i, h)
                for u in units:
                    if TUNITS[u][1] // 4 % 2 == 0:
                        continue
                    t, s, n = TUNITS[u]
                    b = BANK["T", u]
                    wait_full(dve, ("T", u), i, h)
                    nc.vector.tensor_copy(et_slots(t, s, n),
                                          bank[b][:, 0:n * P].rearrange("d (f j q) -> d f j q", f=n, j=NJ)
                                          ).then_inc(bank_empty[b], 1)

            def group(i, h, more=True):
                if more:
                    for k in range(MIDDLE):
                        make_onehot(k, i, h + 1)
                copy_rows(range(NT, 2 * NT), i, h)
                dve.wait_ge(x_hi_ready, i * 2 + (h + 1))
                nc.vector.tensor_tensor(xT_lo[:, :].rearrange("d (j p) -> d j p", j=NJ),
                                        ET[:, :, :, 0].rearrange("d p j -> d j p"),
                                        xT_hi[:, :].bitcast(F32).rearrange("d (j p) -> d j p", j=NJ),
                                        op=ALU.subtract).then_inc(x_lo_ready, 1)
                if more:
                    for k in range(MIDDLE, LATE):
                        make_onehot(k, i, h + 1)
                copy_dots(dve, nc.vector.tensor_copy, dot_units(1, more), i, h)
                dve.wait_ge(z_hi_ready, i * 4 + (2 * h + 1))
                n = NMAIN[0]
                nc.vector.tensor_tensor(zT_lo[0:n, 0:2, :].rearrange("m a (j p) -> m a j p", j=NJ), zt_main(),
                                        zT_hi[0:n, 0:2, :].bitcast(F32).rearrange("m a (j p) -> m a j p", j=NJ),
                                        op=ALU.subtract).then_inc(bank_empty[BANK["ZT", 0]], 1)
                dve.wait_ge(z_hi_ready, i * 4 + (2 * h + 2))
                for a, (r0, r1) in enumerate(REST_ROWS):
                    last = nc.vector.tensor_tensor(zT_lo[r0:r1, 2, :].rearrange("m (j p) -> m j p", j=NJ), zt_rest(a),
                                                   zT_hi[r0:r1, 2, :].bitcast(F32).rearrange("m (j p) -> m j p", j=NJ),
                                                   op=ALU.subtract)
                last.then_inc(bank_empty[BANK["ZT", 1]], 1)
                if more:
                    for k in range(LATE, NX):
                        make_onehot(k, i, h + 1)
                def h1_lo(u):
                    dve.wait_ge(h1_hi_ready, i * 4 + (2 * h + u + 1))
                    half = slice(2 * u, 2 * u + 2)
                    nc.vector.tensor_tensor(h1T_lo[:, half, :], h1T[:, half, :], h1T_hi[:, half, :].bitcast(F32),
                                            op=ALU.subtract).then_inc(h1_lo_ready, 1)

                h1_lo(0)
                wait_full(dve, ("L1", 1), i, h)
                for m in (2, 3):
                    last = nc.vector.tensor_scalar(h1T[:, m, :], l1_out(m), b1_sb[:, m:m + 1], 0.0,
                                                   op0=ALU.add, op1=ALU.max)
                last.then_inc(bank_empty[BANK["L1", 1]], 1)
                h1_lo(1)
                if more:
                    copy_rows(T_FILL["L1"], i, h + 1)
                if more:
                    wait_copied(dve, [("L2", 0)], i, h)
                    nc.vector.tensor_scalar(h2T[:, 0, :], h2T[:, 0, :], w3_sb[:, 0:1], None, op0=ALU.mult
                                            ).then_inc(h2_first, 1)
                b = BANK["L2", 1]
                wait_full(dve, ("L2", 1), i, h)
                nc.vector.tensor_scalar(h2T[:, 1, :], bank[b][:, 0:GROUP], b2_sb[:, 1:2], 0.0,
                                        op0=ALU.add, op1=ALU.max).then_inc(bank_empty[b], 1)
                if more:
                    dve.wait_ge(h2_first, i * 2 + (h + 1))
                    wait_copied(dve, [("L2", 1)], i, h)
                    nc.vector.scalar_tensor_tensor(h2T[:, 1, :], h2T[:, 1, :], w3_sb[:, 1:2], h2T[:, 0, :],
                                                   op0=ALU.mult, op1=ALU.add).then_inc(h2_weighted, 1)
                if more:
                    copy_rows(T_FILL["L2"], i, h + 1)

            nc.vector.memset(ones[:, :], 1.0)
            dve.wait_ge(consts_loaded, 32)
            for n in range(NX):
                make_onehot(n, 0, 0, first=True)
                dve.wait_ge(hi_ready, n + 1)
                nc.vector.tensor_tensor(table_lo[0:VP, n, :], raw[0:VP, n % STAGE, :],
                                        table_hi[0:VP, n, :].bitcast(F32), op=ALU.subtract).then_inc(lo_ready, 1)
                if n > 0:
                    copy_rows(PROLOGUE_T[n - 1], 0, 0)
            copy_rows(PROLOGUE_T[NX - 1], 0, 0)
            dve.wait_ge(w1_loaded, 16 * 3)
            nc.vector.tensor_tensor(w1a_raw, w1a_raw, w1b_raw, op=ALU.add).then_inc(w1d_sum, 1)
            dve.wait_ge(lo_ready, NX)
            nc.vector.memset(Z[:, :, :], 0.0)
            dve.wait_ge(w1_hi_ready, 1)
            nc.vector.tensor_tensor(w1p_lo[:, :, :], w1p_raw[:, :, :], w1p_hi[:, :, :].bitcast(F32), op=ALU.subtract)
            dve.wait_ge(w1_hi_ready, 2)
            nc.vector.tensor_tensor(w1d_lo[:, :], w1a_raw, w1d_hi[:, :].bitcast(F32),
                                    op=ALU.subtract).then_inc(w1_ready, 1)
            dve.wait_ge(w2_hi_ready, 1)
            nc.vector.tensor_tensor(w2_lo[:, :, :], w2_raw, w2_hi[:, :, :].bitcast(F32),
                                    op=ALU.subtract).then_inc(w2_ready, 1)
            with dve.Fori(0, NGROUP // 2 - 1) as i:
                group(i, 0)
                group(i, 1)
            group(NGROUP // 2 - 1, 0)
            group(NGROUP // 2 - 1, 1, more=False)


def _pair_row(a, b):
    f, g = min(a, b), max(a, b)
    return D + NF + f * (2 * NF - f - 1) // 2 + g - f - 1


def kernel(**inputs):
    import numpy as np
    import concourse.bacc as bacc
    from concourse.bass_utils import run_bass_kernel_spmd

    ids = np.ascontiguousarray(inputs["ids"])
    w1 = np.ascontiguousarray(inputs["W_top1"])
    w1p = np.zeros((len(CHUNK) * P, H1), w1.dtype)
    for a in range(NF):
        pairs = [D + ORDER[b] if a == 0 else _pair_row(ORDER[a - 1], ORDER[b]) for b in range(a, NF)]
        if a in MAIN[a % 2]:
            first = P * (a % 2) + OFF[a]
        else:
            first = 2 * P + OFF[a] - NMAIN[0]
        w1p[first:first + len(pairs)] = w1[pairs]
    vid = (VC * np.arange(P)[:, None] + np.arange(VC)[None, :]).astype(np.float32)
    host = {
        "dense": np.ascontiguousarray(inputs["r_dense_features"]).reshape(BATCH // P, P, D),
        "idx": np.ascontiguousarray(ids[:, GATHERED]).reshape(BATCH // P, P, NG),
        "rows": np.ascontiguousarray(ids[:, PICKED].T.reshape(NX, NGROUP, TILES, NJ, NQ).transpose(0, 1, 3, 2, 4)
                                     ).reshape(1, NX, BATCH),
        "w1p": w1p,
        "w1a": np.ascontiguousarray(w1[:D]),
        "w1b": np.ascontiguousarray(w1[-D:]),
        "b1": np.ascontiguousarray(np.asarray(inputs["b_top1"]).reshape(M1, P).T),
        "w2": np.ascontiguousarray(inputs["W_top2"]),
        "b2": np.ascontiguousarray(np.asarray(inputs["b_top2"]).reshape(M2, P).T),
        "w3": np.ascontiguousarray(np.asarray(inputs["W_top3"]).reshape(M2, P).T),
        "ident": np.eye(P, dtype=np.float32),
        "vid": vid,
    }
    for f in range(NF):
        host[f"tbl_{f}"] = np.ascontiguousarray(inputs[f"tbl_{f}"])
    nc = bacc.Bacc("TRN2", target_bir_lowering=False, num_devices=1)
    ap = {k: nc.dram_tensor(f"in_{k}", a.shape, mybir.dt.from_np(a.dtype), kind="ExternalInput").ap()
          for k, a in host.items()}
    y = nc.dram_tensor("y", (BATCH,), F32, kind="ExternalOutput").ap()
    build(nc, ap["dense"], ap["idx"].bitcast(U32), ap["rows"],
          [ap[f"tbl_{f}"] for f in GATHERED], [ap[f"tbl_{f}"] for f in PICKED],
          ap["w1p"], ap["w1a"], ap["w1b"], ap["b1"], ap["w2"], ap["b2"], ap["w3"], ap["ident"], ap["vid"], y)
    r = run_bass_kernel_spmd(nc, [{f"in_{k}": a for k, a in host.items()}], core_ids=[0])
    return r.results[0]["y"].reshape(BATCH, 1)
```
